# Optimizing a Trainium2 kernel written in Bass

```python
import numpy as np
import jax
import jax.numpy as jnp

def _softmax(x, axis=-1):
    return jax.nn.softmax(x, axis=axis)

def _gelu(x):
    return jax.nn.gelu(x, approximate=True)

def _silu(x):
    return jax.nn.silu(x)

def _sigmoid(x):
    return jax.nn.sigmoid(x)

def _layernorm(x, axis=-1, eps=1e-05):
    m = jnp.mean(x, axis=axis, keepdims=True)
    v = jnp.var(x, axis=axis, keepdims=True)
    return (x - m) / jnp.sqrt(v + eps)

def _scatter_add(tgt, idx, src, axis=0):
    return tgt.at[idx].add(src)

def _segment_sum(src, seg, n):
    return jax.ops.segment_sum(src, seg, n)
kernel_name = 'mk_xattn_ffn_d1_seqx_r8_f5614c'

def setup_inputs(seed: int=0):
    np.random.seed(seed)
    _w = jnp.asarray

    def _rec_inputs():
        import jax
        import jax.numpy as jnp
        _rk = jax.random.key(seed)
        x = -0.0003929 + 0.9999 * jax.random.normal(jax.random.fold_in(_rk, 1), (4, 256, 256), jnp.float32)
        _lenS = 256 - jax.random.randint(jax.random.fold_in(_rk, 7), (4,), 0, max(1, 256 // 4) + 1, jnp.int32)
        _lenS2 = 256 - jax.random.randint(jax.random.fold_in(_rk, 8), (4,), 0, max(1, 256 // 4) + 1, jnp.int32)
        _ctx_2048P = jax.random.normal(jax.random.fold_in(_rk, 11), (4, 16, 256), jnp.float32)
        _ctx_2048c = jax.random.dirichlet(jax.random.fold_in(_rk, 511), 0.3 * jnp.ones((16,), jnp.float32), (4, 256))
        _ctx_2048t = jnp.einsum('bsk,bkd->bsd', _ctx_2048c, _ctx_2048P)
        _ctx_2048t = _ctx_2048t * jax.lax.rsqrt(jnp.mean(jnp.square(_ctx_2048t)) + 1e-12) * 0.953939
        ctx_2048 = -0.000514642 + 1.00011 * (_ctx_2048t + 0.3 * jax.random.normal(jax.random.fold_in(_rk, 611), (4, 256, 256), jnp.float32))
        return (x, ctx_2048)
    x, ctx_2048 = _rec_inputs()

    def _L0_xattn_setup():
        import jax, jax.numpy as jnp
        import numpy as np
        DIM = 256
        NHEADS = 32
        HEAD_DIM = DIM // NHEADS
        EPS = 1e-06

        def _rmsnorm(t):
            return t * jax.lax.rsqrt(jnp.mean(t * t, axis=-1, keepdims=True) + EPS)
        key = jax.random.key(seed)
        kx, kc, kq, kk, kv = jax.random.split(key, 5)
        x = jax.random.normal(kx, (2, 512, DIM), dtype=jnp.float32)
        context = jax.random.normal(kc, (2, 64, DIM), dtype=jnp.float32)
        std = 0.02
        Wq = jax.random.normal(kq, (DIM, DIM), dtype=jnp.float32) * std
        Wk = jax.random.normal(kk, (DIM, DIM), dtype=jnp.float32) * std
        Wv = jax.random.normal(kv, (DIM, DIM), dtype=jnp.float32) * std
        return {'x': x, 'context': context, 'Wq': Wq, 'Wk': Wk, 'Wv': Wv}
    _L0_xattn_all = _L0_xattn_setup()
    _L0_xattn_in = {k: v for k, v in _L0_xattn_all.items() if k in ('Wq', 'Wk', 'Wv')}
    del _L0_xattn_all

    def _L0_ffn_setup():
        import jax, jax.numpy as jnp
        import numpy as np
        B, S, H = (2, 256, 256)
        I = 512
        E = 8
        TOP_K = 4
        key = jax.random.key(seed)
        k0, k1, k2, k3, k4 = jax.random.split(key, 5)
        scale = 0.02
        return {'hidden_states': jax.random.normal(k0, (B, S, H), dtype=jnp.float32), 'router_w': jax.random.normal(k1, (H, E), dtype=jnp.float32) * scale, 'w1': jax.random.normal(k2, (E, H, I), dtype=jnp.float32) * scale, 'w2': jax.random.normal(k3, (E, I, I), dtype=jnp.float32) * scale, 'w3': jax.random.normal(k4, (E, I, H), dtype=jnp.float32) * scale}
    _L0_ffn_all = _L0_ffn_setup()
    _L0_ffn_in = {k: v for k, v in _L0_ffn_all.items() if k in ('router_w', 'w1', 'w2', 'w3')}
    del _L0_ffn_all
    return {'x': x, 'ctx_2048': ctx_2048, 'L0_xattn_Wq': _L0_xattn_in['Wq'], 'L0_xattn_Wk': _L0_xattn_in['Wk'], 'L0_xattn_Wv': _L0_xattn_in['Wv'], 'L0_ffn_router_w': _L0_ffn_in['router_w'], 'L0_ffn_w1': _L0_ffn_in['w1'], 'L0_ffn_w2': _L0_ffn_in['w2'], 'L0_ffn_w3': _L0_ffn_in['w3']}

def reference(x, ctx_2048, L0_xattn_Wq, L0_xattn_Wk, L0_xattn_Wv, L0_ffn_router_w, L0_ffn_w1, L0_ffn_w2, L0_ffn_w3):
    import jax
    import jax.numpy as jnp

    def _L0_xattn_ref(x, context, Wq, Wk, Wv):
        import jax, jax.numpy as jnp
        import numpy as np
        DIM = 256
        NHEADS = 32
        HEAD_DIM = DIM // NHEADS
        EPS = 1e-06

        def _rmsnorm(t):
            return t * jax.lax.rsqrt(jnp.mean(t * t, axis=-1, keepdims=True) + EPS)
        b, n, _ = x.shape
        m = context.shape[1]
        q = x @ Wq.T
        k_raw = context @ Wk.T
        v_raw = context @ Wv.T
        q = q.reshape(b, n, NHEADS, HEAD_DIM).transpose(0, 2, 1, 3)
        kv = jnp.concatenate([k_raw, v_raw], axis=-1)
        kv = kv.reshape(b, m, NHEADS, HEAD_DIM, 2)
        k = kv[..., 0].transpose(0, 2, 1, 3)
        v = kv[..., 1].transpose(0, 2, 1, 3)
        q = _rmsnorm(q)
        k = _rmsnorm(k)
        scale = HEAD_DIM ** (-0.5)
        scores = jnp.einsum('bhnd,bhmd->bhnm', q, k) * scale
        attn = jax.nn.softmax(scores, axis=-1)
        out = jnp.einsum('bhnm,bhmd->bhnd', attn, v)
        return out.transpose(0, 2, 1, 3).reshape(b, n, NHEADS * HEAD_DIM)

    def _L0_ffn_ref(hidden_states, router_w, w1, w2, w3):
        import jax, jax.numpy as jnp
        import numpy as np
        B, S, H = (2, 256, 256)
        I = 512
        E = 8
        TOP_K = 4
        b, s, h = hidden_states.shape
        x = hidden_states.reshape(-1, h)
        T = x.shape[0]
        router_logits = x @ router_w
        router_probs = jax.nn.softmax(router_logits, axis=-1)
        top_k_probs, top_k_idx = jax.lax.top_k(router_probs, TOP_K)
        top_k_probs = top_k_probs / jnp.sum(top_k_probs, axis=-1, keepdims=True)
        gates = jnp.zeros((T, E), dtype=x.dtype)
        gates = gates.at[jnp.arange(T)[:, None], top_k_idx].add(top_k_probs)
        h1 = jax.nn.silu(jnp.einsum('th,ehi->eti', x, w1))
        h2 = jax.nn.silu(jnp.einsum('eti,eij->etj', h1, w2))
        out_e = jnp.einsum('etj,ejh->eth', h2, w3)
        out = jnp.einsum('eth,te->th', out_e, gates)
        return out.reshape(b, s, h)
    x = x + _L0_xattn_ref(_layernorm(x, axis=-1), ctx_2048, L0_xattn_Wq, L0_xattn_Wk, L0_xattn_Wv)
    x = x + _L0_ffn_ref(_layernorm(x, axis=-1), L0_ffn_router_w, L0_ffn_w1, L0_ffn_w2, L0_ffn_w3)
    return x

_drawn_inputs = setup_inputs


def setup_inputs(seed=0):
    import zlib

    import numpy as np

    out = dict(_drawn_inputs(seed))
    spreads = {}
    factors = {'L0_ffn_router_w': 8.0, 'L0_ffn_w1': 6.723, 'L0_ffn_w2': 6.649, 'L0_ffn_w3': 6.636}
    for name, (base, spread) in spreads.items():
        noise = np.random.default_rng([zlib.crc32(name.encode()), seed]).standard_normal(out[name].shape)
        drawn = base * np.exp(spread * noise) if base else spread * noise
        out[name] = jnp.asarray(drawn.astype(out[name].dtype))
    for name, factor in factors.items():
        out[name] = (out[name] * factor).astype(out[name].dtype)
    return out
```

```python
from contextlib import ExitStack

import concourse.bass as bass
import concourse.mybir as mybir

F32 = mybir.dt.float32
F32R = mybir.dt.float32r
I32 = mybir.dt.int32
ALU = mybir.AluOpType
ACT = mybir.ActivationFunctionType
AX = mybir.AxisListType.X

B, N, D = 4, 256, 256
P = 128
H, HD = 32, 8
TPB = N // P
T = B * TPB
KD = D // P
HQ = 4
Q = H // HQ
STRIP = 32
E, I, TOP = 8, 512, 4
KI = I // P
HALF = B * N // 2
HT = HALF // P
LN_EPS, RMS_EPS = 1e-5, 1e-6
SCALE = float(HD) ** -0.5
MAGIC = float(0x5F3759DF)
NEWTON = 3

W1C, W2C, W3C = KD * I, KI * I, KI * D
SPLIT = 512
A0 = 3
A_USES, C_USES = 5, 5


class Links:

    def __init__(self, eng, sem):
        self.eng, self.sem, self.n = eng, sem, 0

    def mark(self, ins):
        ins.then_inc(self.sem, 1)
        self.n += 1
        return self.n

    def wait(self, value):
        self.eng.wait_ge(self.sem, value)

    def after(self, ins):
        self.wait(self.mark(ins))


def build(nc, x, ctx, Wq, Wk, Wv, rw, w1, w2, w3, out):
    es = ExitStack()

    def sb(name, cols, dt=F32):
        return es.enter_context(nc.sbuf_tensor(name, [P, *cols], dt))

    def sem(name):
        return es.enter_context(nc.semaphore(name))

    with es:
        ident = sb("ident", [P])
        x_sb = sb("x_sb", [T, D])
        ctx_sb = sb("ctx_sb", [TPB, D])
        w_raw = sb("w_raw", [3, TPB, D])
        wT = sb("wT", [3, KD, D])
        rw_sb = sb("rw_sb", [KD, P])
        rw_hi, rw_lo = sb("rw_hi", [KD, P], F32R), sb("rw_lo", [KD, P], F32R)
        before = sb("before", [E, E])
        stats1, mv1 = sb("stats1", [T, 6]), sb("mv1", [T, 2])
        a1, y1, t1 = sb("a1", [T]), sb("y1", [T]), sb("t1", [T])
        stats2, mv2 = sb("stats2", [TPB, 6]), sb("mv2", [TPB, 2])
        a2, y2, t2 = sb("a2", [TPB]), sb("y2", [TPB]), sb("t2", [TPB])
        ssq = sb("ssq", [2, TPB * H])
        a3, y3, t3 = sb("a3", [2, TPB * H]), sb("y3", [2, TPB * H]), sb("t3", [2, TPB * H])
        xn = sb("xn", [TPB, D])
        xT, cT = sb("xT", [KD, N]), sb("cT", [KD, N])
        q_sb = sb("q_sb", [TPB, D])
        kv_sb = sb("kv_sb", [TPB, 2 * D])
        tmp = sb("tmp", [2, TPB * D])
        big = [sb(f"big{i}", [4, I], F32R) for i in range(4)]
        qk_part = [big[i][:].rearrange("p a b -> p (a b)").rearrange("p (j x) -> p j x", j=TPB) for i in range(2)]
        qkT = [big[2 + i] for i in range(2)]
        v_ext = sb("v_ext", [TPB, H, STRIP])
        probs = sb("probs", [2, HQ, TPB * N])
        oT = sb("oT", [Q, N])
        r_den = sb("r_den", [4, H // 2])
        att = sb("att", [TPB, D])
        x2n = sb("x2n", [TPB, D])
        acc = sb("acc", [T, D])
        x2T_hi, x2T_lo = sb("x2T_hi", [KD, T * P], F32R), sb("x2T_lo", [KD, T * P], F32R)
        logT = sb("logT", [T * P])
        logits = sb("logits", [T, E])
        row = sb("row", [4, T])
        pr = sb("pr", [T, E])
        gt = sb("gt", [T * E, E])
        eq = sb("eq", [T * E, E])
        gates = sb("gates", [T, E])
        raw = sb("raw", [W1C + W2C + W3C])
        w_hi, w_lo = sb("w_hi", [W1C + W2C + W3C], F32R), sb("w_lo", [W1C + W2C + W3C], F32R)
        silu = sb("silu", [4, HALF])
        h1_hi, h1_lo, h2_hi, h2_lo = big[0], big[1], big[2], big[3]

        s_bank = [es.enter_context(nc.psum_tensor(f"s_bank{i}", [P, 512], F32)) for i in range(4)]
        pv_bank = es.enter_context(nc.psum_tensor("pv_bank", [P, 512], F32))
        bank_a = es.enter_context(nc.psum_tensor("bank_a", [P, 512], F32))
        bank_b = es.enter_context(nc.psum_tensor("bank_b", [P, 512], F32))
        bank_c = es.enter_context(nc.psum_tensor("bank_c", [P, 512], F32))
        out_bank = [bank_b, bank_a]

        x_in, x_rest_in, ctx_in, wqkv_in, rw_in = sem("x_in"), sem("x_rest_in"), sem("ctx_in"), sem("wqkv_in"), sem("rw_in")
        w_in = [sem("w1_in"), sem("w2_in"), sem("w3_in")]
        ident_ready, v_const_ready, mask_ready = sem("ident_ready"), sem("v_const_ready"), sem("mask_ready")
        pool_zeroed = sem("pool_zeroed")
        dve_step, pool_step, act_step = sem("dve_step"), sem("pool_step"), sem("act_step")
        a_full, a_free = sem("a_full"), sem("a_free")
        b_full, b_free = sem("b_full"), sem("b_free")
        c_full, c_free = sem("c_full"), sem("c_free")
        mv1_ready, rstd1_ready, xn_ready = sem("mv1_ready"), sem("rstd1_ready"), sem("xn_ready")
        ssq_ready, rrms_ready, parts_ready, v_ready = sem("ssq_ready"), sem("rrms_ready"), sem("parts_ready"), sem("v_ready")
        normed, hi_ready = sem("normed"), sem("hi_ready")
        s_full, exp_done, pv_done, pv_free = sem("s_full"), sem("exp_done"), sem("pv_done"), sem("pv_free")
        mv2_ready, rstd2_ready, x2n_ready, x2T_ready = sem("mv2_ready"), sem("rstd2_ready"), sem("x2n_ready"), sem("x2T_ready")
        rw_split, gates_ready, shifted, exped = sem("rw_split"), sem("gates_ready"), sem("shifted"), sem("exped")
        w_hi_ready, w_lo_ready = [sem(f"w{m}_hi_ready") for m in (1, 2, 3)], [sem(f"w{m}_lo_ready") for m in (1, 2, 3)]
        z_full, rw_zeroed = sem("z_full"), sem("rw_zeroed")
        silu_ready, h_hi_ready, h_ready = sem("silu_ready"), sem("h_hi_ready"), sem("h_ready")
        o_full, o_free, out_done = sem("o_full"), sem("o_free"), sem("out_done")
        block = es.enter_context(nc.Block())

        tmps = [tmp[:, s, :].rearrange("p (r d) -> p r d", d=HD) for s in range(2)]

        def twice(v):
            return v.unsqueeze(2).to_broadcast([P, TPB * H, 2, HD])

        def part(s, lo):
            v = qk_part[s].rearrange("p j (h x) -> p (j h) x", x=STRIP)
            if s == 0:
                return v.rearrange("p r (c s d) -> p r c s d", s=2, d=HD)[:, :, :, lo, :]
            return v.rearrange("p r (s c d) -> p r s c d", s=2, d=HD)[:, :, lo, :, :]

        W_OFF = [0, W1C, W1C + W2C]
        W_COLS = [W1C, W2C, W3C]
        W_STEPS = [c // SPLIT for c in W_COLS]

        def parts_read(m, e):
            return ((z_full, 16 * e + 12), (z_full, 16 * e + 16), (o_full, T * (e + 1)))[m]

        @block.sync
        def _(sp):
            sp.dma_start(x_sb[:, 0:TPB, :], x[0].rearrange("(j p) d -> p j d", p=P)).then_inc(x_in, 16)
            sp.dma_start(w_raw[:, 0], Wq.rearrange("(o p) d -> p o d", p=P)).then_inc(wqkv_in, 16)
            sp.dma_start(w_raw[:, 1], Wk.rearrange("(o p) d -> p o d", p=P)).then_inc(wqkv_in, 16)
            sp.dma_start(w_raw[:, 2], Wv.rearrange("(o p) d -> p o d", p=P)).then_inc(wqkv_in, 16)
            sp.wait_ge(rw_zeroed, 1)
            sp.dma_start(rw_sb[:, :, 0:E], rw.rearrange("(k p) e -> p k e", p=P)).then_inc(rw_in, 16)

            def load_expert(e):
                for m, (w, k, width) in enumerate(((w1, KD, I), (w2, KI, I), (w3, KI, D))):
                    if not (isinstance(e, int) and e == 0):
                        sp.wait_ge(w_hi_ready[m], e * W_STEPS[m])
                        sp.wait_ge(w_lo_ready[m], e * W_STEPS[m])
                    src = w[bass.ds(e, 1)].rearrange("a (k p) n -> p (a k) n", p=P)
                    dst = raw[:, W_OFF[m]:W_OFF[m] + W_COLS[m]].rearrange("p (k n) -> p k n", n=width)
                    sp.dma_start(dst, src).then_inc(w_in[m], 16)

            load_expert(0)
            for b in range(1, B):
                sp.wait_ge(a_full, A0 + A_USES * (b - 1) + 2)
                sp.dma_start(ctx_sb[:], ctx[b].rearrange("(j p) d -> p j d", p=P)).then_inc(ctx_in, 16)
            with sp.Fori(1, E) as e:
                load_expert(e)
            for t in range(T):
                sp.wait_ge(o_free, (E - 1) * T + t + 1)
                sp.dma_start(out[t // TPB, (t % TPB) * P:(t % TPB + 1) * P, :], acc[:, t, :]).then_inc(out_done, 16)
            sp.wait_ge(out_done, 16 * T)

        @block.gpsimd
        def _(pool):
            links = Links(pool, pool_step)
            pool.memset(rw_sb[:], 0.0).then_inc(rw_zeroed, 1)
            pool.memset(ident[:], 0.0).then_inc(pool_zeroed, 1)
            pool.wait_ge(pool_zeroed, 1)
            pool.affine_select(out=ident[:], in_=ident[:], compare_op=ALU.not_equal, fill=1.0, base=0,
                               pattern=[[-1, P]], channel_multiplier=1).then_inc(ident_ready, 1)
            links.after(pool.memset(v_ext[:], 0.0))
            pool.memset(v_ext[:, :, :, HD:HD + 1], 1.0).then_inc(v_const_ready, 1)
            links.after(pool.memset(before[:], 0.0))
            for i in range(1, E):
                pool.memset(before[:, i, 0:i], 1.0).then_inc(mask_ready, 1)

            def rsqrt(a, y, t, src, mul, eps, done):
                links.after(pool.tensor_scalar(a, src, mul, eps, ALU.mult, ALU.add))
                links.after(pool.tensor_scalar(y.bitcast(I32), a.bitcast(I32), -0.5, MAGIC, ALU.mult, ALU.add))
                for n in range(NEWTON):
                    links.after(pool.tensor_tensor(t, y, y, ALU.mult))
                    links.after(pool.tensor_tensor(t, t, a, ALU.mult))
                    links.after(pool.tensor_scalar(t, t, -0.5, 1.5, ALU.mult, ALU.add))
                    last = pool.tensor_tensor(y, y, t, ALU.mult)
                    if n < NEWTON - 1:
                        links.after(last)
                last.then_inc(done, 1)

            def rms(b):
                pool.wait_ge(ssq_ready, 2 * (b + 1))
                rsqrt(a3[:], y3[:], t3[:], ssq[:], 1.0 / HD, RMS_EPS, rrms_ready)

            def round_qk(b):
                if b > 0:
                    pool.wait_ge(b_full, Q * b)
                for s in range(2):
                    pool.wait_ge(normed, 2 * b + s + 1)
                    pool.tensor_scalar(part(s, 0), twice(tmps[s]), 1.0, 0.0, ALU.mult, ALU.add).then_inc(hi_ready, 1)

            def values(b):
                pool.wait_ge(a_free, A0 + A_USES * b + 4)
                if b == 0:
                    pool.wait_ge(v_const_ready, 1)
                else:
                    pool.wait_ge(pv_done, Q * b)
                for c in range(TPB):
                    v = kv_sb[:, c, :].rearrange("p (h d s) -> p h d s", d=HD, s=2)[:, :, :, 1]
                    pool.tensor_scalar(v_ext[:, c, :, 0:HD], v, 1.0, 0.0, ALU.mult, ALU.add).then_inc(v_ready, 1)

            def norm2(b):
                pool.wait_ge(mv2_ready, TPB * (b + 1))
                rsqrt(a2[:], y2[:], t2[:], mv2[:, :, 1], 1.0, LN_EPS, rstd2_ready)

            def split(m):
                pool.wait_ge(w_in[m], 16)
                for s in range(W_STEPS[m]):
                    cols = slice(W_OFF[m] + s * SPLIT, W_OFF[m] + (s + 1) * SPLIT)
                    pool.tensor_scalar(w_hi[:, cols], raw[:, cols], 1.0, 0.0, ALU.mult, ALU.add).then_inc(w_hi_ready[m], 1)

            pool.wait_ge(mv1_ready, T)
            rsqrt(a1[:], y1[:], t1[:], mv1[:, :, 1], 1.0, LN_EPS, rstd1_ready)
            rms(0)
            round_qk(0)
            values(0)

            def step(b, first=False, last=False):
                if not last:
                    rms(b + 1)
                if not first:
                    norm2(b - 1)
                if not last:
                    round_qk(b + 1)
                    values(b + 1)

            step(0, first=True)
            for b in range(1, B):
                step(b, last=(b == B - 1))
            for m in range(3):
                split(m)
            norm2(B - 1)

        @block.scalar
        def _(act):
            act.dma_start(ctx_sb[:], ctx[0].rearrange("(j p) d -> p j d", p=P)).then_inc(ctx_in, 16)
            act.dma_start(x_sb[:, TPB:, :].rearrange("p (b j) d -> p b j d", j=TPB),
                          x[1:].rearrange("b (j p) d -> p b j d", p=P)).then_inc(x_rest_in, 16)

            def exps(b):
                for g in range(Q):
                    if not (b == 0 and g < 2):
                        act.wait_ge(pv_done, Q * b + g - 1)
                    for r in range(HQ):
                        act.wait_ge(s_full, HQ * (Q * b + g) + r + 1)
                        act.activation(probs[:, g % 2, r, :], s_bank[r][:], ACT.Exp, scale=SCALE).then_inc(exp_done, 1)

            for b in range(B):
                exps(b)

            def hidden(first, hi):
                for m in range(KI):
                    act.wait_ge(z_full, first + m + 1)
                    if not (isinstance(first, int) and first == 0):
                        act.wait_ge(h_ready, first + m - 3)
                    act.activation(silu[:, m, :], s_bank[m][:], ACT.Silu).then_inc(silu_ready, 1)
                    act.activation(hi[:, m, :], s_bank[m][:], ACT.Silu).then_inc(h_hi_ready, 1)

            def split(m, e):
                act.wait_ge(w_in[m], 16 * (e + 1))
                act.wait_ge(*parts_read(m, e - 1))
                for s in range(W_STEPS[m]):
                    cols = slice(W_OFF[m] + s * SPLIT, W_OFF[m] + (s + 1) * SPLIT)
                    act.activation(w_hi[:, cols], raw[:, cols], ACT.Copy).then_inc(w_hi_ready[m], 1)

            def expert(e, last=False):
                hidden(16 * e + 4, h2_hi)
                hidden(16 * e + 8, h1_hi)
                if not last:
                    split(0, e + 1)
                hidden(16 * e + 12, h2_hi)
                if not last:
                    hidden(16 * e + 16, h1_hi)
                    split(1, e + 1)
                    split(2, e + 1)

            act.wait_ge(shifted, 1)
            act.activation(pr[:], pr[:], ACT.Exp).then_inc(exped, 1)
            hidden(0, h1_hi)
            expert(0)
            with act.Fori(1, E - 1) as e:
                expert(e)
            expert(E - 1, last=True)

        @block.vector
        def _(dve):
            links = Links(dve, dve_step)

            def evac_a(b, k, dst):
                if k in (2, 3) and b > 0:
                    dve.wait_ge(v_ready, TPB * b)
                dve.wait_ge(a_full, A0 + A_USES * b + k + 1)
                dve.tensor_copy(dst, bank_a[:]).then_inc(a_free, 1)

            def x_norm(b):
                for j in range(TPB):
                    t = TPB * b + j
                    dve.tensor_scalar(xn[:, j, :], x_sb[:, t, :],
                                      mv1[:, t, 0:1], y1[:, t:t + 1],
                                      ALU.subtract, ALU.mult).then_inc(xn_ready, 1)

            q_in = q_sb[:].rearrange("p j (h d) -> p (j h) d", d=HD)
            k_in = kv_sb[:].rearrange("p c (h d s) -> p (c h) d s", d=HD, s=2)[:, :, :, 0]

            def squares(b):
                dve.wait_ge(a_free, A0 + A_USES * (b + 1))
                marks = []
                for s, v in enumerate((q_in, k_in)):
                    marks.append(links.mark(dve.tensor_tensor(tmps[s], v, v, ALU.mult)))
                for s in range(2):
                    links.wait(marks[s])
                    dve.tensor_reduce(ssq[:, s, :], tmps[s], AX, ALU.add).then_inc(ssq_ready, 1)

            def parts(b):
                dve.wait_ge(rrms_ready, b + 1)
                for s, v in enumerate((q_in, k_in)):
                    r = y3[:, s, :].unsqueeze(2).to_broadcast([P, TPB * H, HD])
                    dve.tensor_tensor(tmps[s], v, r, ALU.mult).then_inc(normed, 1)
                for s in range(2):
                    dve.wait_ge(hi_ready, 2 * b + s + 1)
                    dve.tensor_tensor(part(s, 1), twice(tmps[s]), part(s, 0).bitcast(F32), ALU.subtract).then_inc(parts_ready, 1)

            def evac_b(b, g):
                dve.wait_ge(b_full, Q * b + g + 1)
                if b > 0:
                    dve.wait_ge(s_full, HQ * (Q * (b - 1) + g + 1))
                dve.tensor_copy(qkT[g // 4][:, g % 4, :], bank_b[:]).then_inc(b_free, 1)

            def evac_pv(b, g):
                dve.wait_ge(pv_done, Q * b + g + 1)
                dve.tensor_copy(oT[:, g, :], pv_bank[:, 0:N]).then_inc(pv_free, 1)

            def divide(b, half, j):
                use = 2 * half + j
                dve.wait_ge(c_full, C_USES * b + use + 1)
                o = bank_c[:].rearrange("p (h s) -> p h s", s=STRIP)
                links.after(dve.reciprocal(r_den[:, use, :], o[:, :, HD]))
                dst = att[:, j, half * P:(half + 1) * P].rearrange("p (h d) -> p h d", d=HD)
                den = r_den[:, use, :].unsqueeze(2).to_broadcast([P, H // 2, HD])
                dve.tensor_tensor(dst, o[:, :, 0:HD], den, ALU.mult).then_inc(c_free, 1)

            def residual(b):
                dve.wait_ge(c_free, C_USES * b + 4)
                tiles = slice(TPB * b, TPB * (b + 1))
                done = links.mark(dve.tensor_tensor(acc[:, tiles, :], att[:], x_sb[:, tiles, :], ALU.add))
                links.wait(done)
                for j in range(TPB):
                    done = links.mark(dve.bn_stats(stats2[:, j, :], acc[:, TPB * b + j, :]))
                links.wait(done)
                for j in range(TPB):
                    dve.bn_aggr(mv2[:, j, :], stats2[:, j, :]).then_inc(mv2_ready, 1)

            def x2_norm(b):
                dve.wait_ge(rstd2_ready, b + 1)
                for j in range(TPB):
                    dve.tensor_scalar(x2n[:, j, :], acc[:, TPB * b + j, :],
                                      mv2[:, j, 0:1], y2[:, j:j + 1], ALU.subtract, ALU.mult).then_inc(x2n_ready, 1)

            def x2_parts(b):
                dve.wait_ge(c_full, C_USES * b + 5)
                cols = slice(N * b, N * (b + 1))
                full = bank_c[:].rearrange("p (k n) -> p k n", k=KD)
                links.after(dve.tensor_copy(x2T_hi[:, :, cols], full))
                dve.tensor_tensor(x2T_lo[:, :, cols], full, x2T_hi[:, :, cols].bitcast(F32), ALU.subtract).then_inc(c_free, 1)

            def split(m, e):
                dve.wait_ge(w_in[m], 16 * (e + 1))
                if not (isinstance(e, int) and e == 0):
                    dve.wait_ge(*parts_read(m, e - 1))
                for s in range(W_STEPS[m]):
                    cols = slice(W_OFF[m] + s * SPLIT, W_OFF[m] + (s + 1) * SPLIT)
                    dve.wait_ge(w_hi_ready[m], W_STEPS[m] * e + s + 1)
                    dve.tensor_tensor(w_lo[:, cols], raw[:, cols], w_hi[:, cols].bitcast(F32),
                                      ALU.subtract).then_inc(w_lo_ready[m], 1)

            def step(b, first=False, last=False):
                for g in range(Q):
                    if g < Q - 1:
                        evac_b(b, g + 1)
                    if g == 0:
                        if not first:
                            divide(b - 1, 0, 0)
                            divide(b - 1, 0, 1)
                        if not last:
                            x_norm(b + 1)
                            evac_a(b + 1, 0, xT[:].rearrange("p k n -> p (k n)"))
                    if g > 0:
                        evac_pv(b, g - 1)
                    if g == 1:
                        if not first:
                            divide(b - 1, 1, 0)
                            divide(b - 1, 1, 1)
                            residual(b - 1)
                        if not last:
                            evac_a(b + 1, 1, cT[:].rearrange("p k n -> p (k n)"))
                    if g == 2 and not last:
                        evac_a(b + 1, 2, kv_sb[:, 0, :])
                        evac_a(b + 1, 3, kv_sb[:, 1, :])
                    if g == 3 and not last:
                        evac_a(b + 1, 4, q_sb[:].rearrange("p j d -> p (j d)"))
                        squares(b + 1)
                    if g == 4 and not first:
                        x2_norm(b - 1)
                    if g == 5 and not first:
                        x2_parts(b - 1)
                    if g == 7 and not last:
                        parts(b + 1)
                    if g >= Q - 3 and last:
                        split(g - (Q - 3), 0)
                evac_pv(b, Q - 1)
                if not last:
                    evac_b(b + 1, 0)

            for t in range(T):
                if t in (0, TPB):
                    dve.wait_ge(x_in if t == 0 else x_rest_in, 16)
                links.mark(dve.bn_stats(stats1[:, t, :], x_sb[:, t, :]))
            for t in range(T):
                if t in (0, TPB):
                    links.wait(links.n if t else TPB)
                dve.bn_aggr(mv1[:, t, :], stats1[:, t, :]).then_inc(mv1_ready, 1)
            for m in range(3):
                dve.wait_ge(a_full, m + 1)
                dve.tensor_copy(wT[:, m].rearrange("p k o -> p (k o)"), bank_a[:]).then_inc(a_free, 1)
            dve.wait_ge(rw_in, 16)
            links.after(dve.tensor_copy(rw_hi[:], rw_sb[:]))
            dve.tensor_tensor(rw_lo[:], rw_sb[:], rw_hi[:].bitcast(F32), ALU.subtract).then_inc(rw_split, 1)
            dve.wait_ge(rstd1_ready, 1)
            x_norm(0)
            evac_a(0, 0, xT[:].rearrange("p k n -> p (k n)"))
            evac_a(0, 1, cT[:].rearrange("p k n -> p (k n)"))
            evac_a(0, 2, kv_sb[:, 0, :])
            evac_a(0, 3, kv_sb[:, 1, :])
            evac_a(0, 4, q_sb[:].rearrange("p j d -> p (j d)"))
            squares(0)
            parts(0)
            evac_b(0, 0)

            step(0, first=True)
            for b in range(1, B):
                step(b, last=(b == B - 1))

            def hidden(first, hi, lo):
                for m in range(KI):
                    dve.wait_ge(silu_ready, first + m + 1)
                    dve.wait_ge(h_hi_ready, first + m + 1)
                    dve.tensor_tensor(lo[:, m, :], silu[:, m, :], hi[:, m, :].bitcast(F32), ALU.subtract).then_inc(h_ready, 1)

            def combine(e, t):
                for j in range(HT):
                    tile = HT * t + j
                    dve.wait_ge(o_full, T * e + tile + 1)
                    dve.scalar_tensor_tensor(acc[:, tile, :], out_bank[j % 2][:, 0:D], gates[:, tile, bass.ds(e, 1)],
                                             acc[:, tile, :], ALU.mult, ALU.add).then_inc(o_free, 1)

            def expert(e, last=False):
                hidden(16 * e + 4, h2_hi, h2_lo)
                hidden(16 * e + 8, h1_hi, h1_lo)
                if not last:
                    split(0, e + 1)
                combine(e, 0)
                hidden(16 * e + 12, h2_hi, h2_lo)
                if not last:
                    hidden(16 * e + 16, h1_hi, h1_lo)
                    split(1, e + 1)
                combine(e, 1)
                if not last:
                    split(2, e + 1)

            def router():
                le = [P, T, E]
                dve.wait_ge(c_full, C_USES * B + 3)
                links.after(dve.tensor_copy(logits[:].rearrange("p t e -> p (t e)"), bank_c[:, 0:T * E]))
                links.after(dve.tensor_reduce(row[:, 0, :], logits[:], AX, ALU.max))
                dve.tensor_tensor(pr[:], logits[:], row[:, 0, :].unsqueeze(2).to_broadcast(le), ALU.subtract).then_inc(shifted, 1)
                dve.wait_ge(exped, 1)
                links.after(dve.tensor_reduce(row[:, 1, :], pr[:], AX, ALU.add))
                links.after(dve.reciprocal(row[:, 2, :], row[:, 1, :]))
                links.after(dve.tensor_tensor(pr[:], pr[:], row[:, 2, :].unsqueeze(2).to_broadcast(le), ALU.mult))
                other = pr[:].unsqueeze(2).to_broadcast([P, T, E, E])
                own = pr[:].unsqueeze(3).to_broadcast([P, T, E, E])
                v4 = lambda m: m[:].rearrange("p (t i) j -> p t i j", i=E)
                links.mark(dve.tensor_tensor(v4(gt), other, own, ALU.is_gt))
                links.after(dve.tensor_tensor(v4(eq), other, own, ALU.is_equal))
                dve.wait_ge(mask_ready, E - 1)
                links.after(dve.tensor_tensor(v4(eq), v4(eq), before[:].unsqueeze(1).to_broadcast([P, T, E, E]), ALU.mult))
                links.after(dve.tensor_tensor(gt[:], gt[:], eq[:], ALU.add))
                flat = gates[:].rearrange("p t e -> p (t e)")
                links.after(dve.tensor_reduce(flat, gt[:], AX, ALU.add))
                links.after(dve.tensor_scalar(flat, flat, float(TOP), None, ALU.is_lt))
                links.after(dve.tensor_tensor(pr[:], pr[:], gates[:], ALU.mult))
                links.after(dve.tensor_reduce(row[:, 3, :], pr[:], AX, ALU.add))
                links.after(dve.reciprocal(row[:, 1, :], row[:, 3, :]))
                links.after(dve.tensor_tensor(gates[:], pr[:], row[:, 1, :].unsqueeze(2).to_broadcast(le), ALU.mult))

            for half, j in ((0, 0), (0, 1), (1, 0), (1, 1)):
                divide(B - 1, half, j)
            residual(B - 1)
            x2_norm(B - 1)
            x2_parts(B - 1)
            for half in range(2):
                dve.wait_ge(c_full, C_USES * B + half + 1)
                dve.tensor_copy(logT[0:E, half * HALF:(half + 1) * HALF], bank_c[0:E, :]).then_inc(c_free, 1)
            router()
            hidden(0, h1_hi, h1_lo)
            expert(0)
            with dve.Fori(1, E - 1) as e:
                expert(e)
            expert(E - 1, last=True)

        @block.tensor
        def _(pe):
            def before_a(b, k):
                pe.wait_ge(a_free, A0 + A_USES * b + k)

            def transpose_a(b, k, src):
                before_a(b, k)
                for j in range(TPB):
                    for c in range(KD):
                        last = pe.transpose(bank_a[:, c * N + j * P:c * N + (j + 1) * P], src[:, j, c * P:(c + 1) * P], ident[:])
                last.then_inc(a_full, 1)

            def x_transpose(b):
                pe.wait_ge(xn_ready, TPB * (b + 1))
                transpose_a(b, 0, xn)

            def ctx_transpose(b):
                pe.wait_ge(ctx_in, 16 * (b + 1))
                transpose_a(b, 1, ctx_sb)

            def project_kv(b, c):
                before_a(b, 2 + c)
                for m in range(2):
                    for k in range(KD):
                        last = pe.matmul(bank_a[:, m * D:(m + 1) * D], cT[:, k, c * P:(c + 1) * P], wT[:, 1 + m, k, :],
                                         start=(k == 0), stop=(k == KD - 1))
                last.then_inc(a_full, 1)

            def project_q(b):
                before_a(b, 4)
                for j in range(TPB):
                    for k in range(KD):
                        last = pe.matmul(bank_a[:, j * D:(j + 1) * D], xT[:, k, j * P:(j + 1) * P], wT[:, 0, k, :],
                                         start=(k == 0), stop=(k == KD - 1))
                last.then_inc(a_full, 1)

            def qk_transpose(b, g):
                if g == 0:
                    pe.wait_ge(parts_ready, 2 * (b + 1))
                if not (b == 0 and g == 0):
                    pe.wait_ge(b_free, Q * b + g)
                for s in range(2):
                    for j in range(TPB):
                        v = qk_part[s][:, j, g * P:(g + 1) * P].bitcast(F32)
                        last = pe.transpose(bank_b[:, s * N + j * P:s * N + (j + 1) * P], v, ident[:])
                last.then_inc(b_full, 1)

            def scores(b, g, pair):
                if pair == 0:
                    pe.wait_ge(b_free, Q * b + g + 1)
                for c in range(TPB):
                    for r in (2 * pair, 2 * pair + 1):
                        if c == 0 and not (b == 0 and g == 0):
                            pe.wait_ge(exp_done, HQ * (Q * b + g - 1) + r + 1)
                        rows = slice(STRIP * r, STRIP * (r + 1))
                        qk = qkT[g // 4][rows, g % 4, :]
                        last = pe.matmul(s_bank[r][:, c * N:(c + 1) * N], qk[:, N + c * P:N + (c + 1) * P], qk[:, 0:N],
                                         start=True, stop=True)
                        if c == TPB - 1:
                            last.then_inc(s_full, 1)

            def values(b, g, c):
                if c == 0:
                    if g == 0:
                        pe.wait_ge(v_ready, TPB * (b + 1))
                    if not (b == 0 and g == 0):
                        pe.wait_ge(pv_free, Q * b + g)
                    pe.wait_ge(exp_done, HQ * (Q * b + g + 1))
                for r in range(HQ):
                    rows = slice(STRIP * r, STRIP * (r + 1))
                    last = pe.matmul(pv_bank[rows, 0:N], v_ext[:, c, HQ * g + r, :], probs[:, g % 2, r, c * N:(c + 1) * N],
                                     start=(c == 0), stop=(c == TPB - 1), tile_position=(0, STRIP * r))
                if c == TPB - 1:
                    last.then_inc(pv_done, 1)

            def before_c(u):
                if u > 0:
                    pe.wait_ge(c_free, u)

            def o_transpose(b, half, j):
                before_c(C_USES * b + 2 * half + j)
                pe.wait_ge(pv_free, Q * b + 4 * (half + 1))
                for g in range(4):
                    last = pe.transpose(bank_c[:, g * P:(g + 1) * P], oT[:, 4 * half + g, j * P:(j + 1) * P], ident[:])
                last.then_inc(c_full, 1)

            def x2_transpose(b):
                pe.wait_ge(x2n_ready, TPB * (b + 1))
                before_c(C_USES * b + 4)
                for j in range(TPB):
                    for k in range(KD):
                        last = pe.transpose(bank_c[:, k * N + j * P:k * N + (j + 1) * P], x2n[:, j, k * P:(k + 1) * P], ident[:])
                last.then_inc(c_full, 1)

            def step(b, first=False, last=False):
                for g in range(Q):
                    scores(b, g, 0)
                    if g < Q - 1:
                        qk_transpose(b, g + 1)
                    if g > 0:
                        values(b, g - 1, 0)
                    if g == 0 and not first:
                        o_transpose(b - 1, 0, 0)
                        o_transpose(b - 1, 0, 1)
                    if g == 0 and not last:
                        x_transpose(b + 1)
                    scores(b, g, 1)
                    if g > 0:
                        values(b, g - 1, 1)
                    if g == 1 and not first:
                        o_transpose(b - 1, 1, 0)
                        o_transpose(b - 1, 1, 1)
                    if not last:
                        if g == 1:
                            ctx_transpose(b + 1)
                        if g == 2:
                            project_kv(b + 1, 0)
                            project_kv(b + 1, 1)
                        if g == 3:
                            project_q(b + 1)
                    if g == 5 and not first:
                        x2_transpose(b - 1)
                values(b, Q - 1, 0)
                values(b, Q - 1, 1)
                if not last:
                    qk_transpose(b + 1, 0)

            pe.wait_ge(ident_ready, 1)
            pe.wait_ge(wqkv_in, 48)
            for m in range(3):
                if m:
                    pe.wait_ge(a_free, m)
                for o in range(TPB):
                    for k in range(KD):
                        last = pe.transpose(bank_a[:, k * D + o * P:k * D + (o + 1) * P], w_raw[:, m, o, k * P:(k + 1) * P], ident[:])
                last.then_inc(a_full, 1)
            x_transpose(0)
            ctx_transpose(0)
            project_kv(0, 0)
            project_kv(0, 1)
            project_q(0)
            qk_transpose(0, 0)
            step(0, first=True)
            for b in range(1, B):
                step(b, last=(b == B - 1))

            def weights(m, k, width, first, cols):
                at = slice(W_OFF[m] + k * width + first, W_OFF[m] + k * width + first + cols)
                return w_hi[:, at], w_lo[:, at]

            def layer(m, e, t, chunk, rhs_hi, rhs_lo, ks, cols):
                for n in range(KI):
                    if not (isinstance(chunk, int) and chunk == 0):
                        pe.wait_ge(h_hi_ready, chunk + n - 3)
                    for k in range(ks):
                        if m == 1 and n == 0:
                            pe.wait_ge(h_ready, chunk + k - 3)
                        hi, lo = weights(m, k, I, n * P, P)
                        for i, (w, r) in enumerate(((hi, rhs_hi), (hi, rhs_lo), (lo, rhs_hi))):
                            last = pe.matmul(s_bank[n][:], w, r[:, k, cols], start=(k == 0 and i == 0),
                                             stop=(k == ks - 1 and i == 2))
                    last.then_inc(z_full, 1)

            def layer1(e, t):
                if t == 0:
                    pe.wait_ge(w_lo_ready[0], W_STEPS[0] * (e + 1))
                layer(0, e, t, 16 * e + 8 * t, x2T_hi, x2T_lo, KD, slice(t * HALF, (t + 1) * HALF))

            def layer2(e, t):
                if t == 0:
                    pe.wait_ge(w_lo_ready[1], W_STEPS[1] * (e + 1))
                layer(1, e, t, 16 * e + 8 * t + 4, h1_hi, h1_lo, KI, slice(0, HALF))

            def layer3(e, t):
                if t == 0:
                    pe.wait_ge(w_lo_ready[2], W_STEPS[2] * (e + 1))
                for j in range(HT):
                    n = T * e + HT * t + j
                    if not (isinstance(n, int) and n < 2):
                        pe.wait_ge(o_free, n - 1)
                    for k in range(KI):
                        if j == 0:
                            pe.wait_ge(h_ready, 16 * e + 8 * t + 4 + k + 1)
                        whi, wlo = weights(2, k, D, 0, D)
                        tok = slice(j * P, (j + 1) * P)
                        for i, (h, w) in enumerate(((h2_hi, whi), (h2_hi, wlo), (h2_lo, whi))):
                            last = pe.matmul(out_bank[j % 2][:, 0:D], h[:, k, tok], w, start=(k == 0 and i == 0),
                                             stop=(k == KI - 1 and i == 2))
                    last.then_inc(o_full, 1)

            def expert(e, last=False):
                layer2(e, 0)
                layer1(e, 1)
                layer3(e, 0)
                layer2(e, 1)
                if not last:
                    layer1(e + 1, 0)
                layer3(e, 1)

            for half, j in ((0, 0), (0, 1), (1, 0), (1, 1)):
                o_transpose(B - 1, half, j)
            x2_transpose(B - 1)
            pe.wait_ge(rw_split, 1)
            for half in range(2):
                before_c(C_USES * B + half)
                for k in range(KD):
                    for i, (w, r) in enumerate(((rw_hi, x2T_hi), (rw_hi, x2T_lo), (rw_lo, x2T_hi))):
                        last = pe.matmul(bank_c[:], w[:, k, :], r[:, k, half * HALF:(half + 1) * HALF],
                                         start=(k == 0 and i == 0), stop=(k == KD - 1 and i == 2))
                last.then_inc(c_full, 1)
            before_c(C_USES * B + 2)
            for t in range(T):
                last = pe.transpose(bank_c[:, t * E:(t + 1) * E], logT[0:E, t * P:(t + 1) * P], ident[0:E, 0:E])
            last.then_inc(c_full, 1)
            layer1(0, 0)
            expert(0)
            with pe.Fori(1, E - 1) as e:
                expert(e)
            expert(E - 1, last=True)


_INS = ['x', 'ctx_2048', 'L0_xattn_Wq', 'L0_xattn_Wk', 'L0_xattn_Wv', 'L0_ffn_router_w', 'L0_ffn_w1', 'L0_ffn_w2', 'L0_ffn_w3']


def kernel(**inputs):
    import numpy as np
    import concourse.bacc as bacc
    from concourse.bass_utils import run_bass_kernel_spmd

    nc = bacc.Bacc("TRN2", target_bir_lowering=False, num_devices=1)
    arrays, args = {}, []
    for name in _INS:
        a = np.ascontiguousarray(inputs[name])
        arrays[f"in_{name}"] = a
        args.append(nc.dram_tensor(f"in_{name}", a.shape, mybir.dt.from_np(a.dtype), kind="ExternalInput").ap())
    out = nc.dram_tensor("out", (B, N, D), F32, kind="ExternalOutput").ap()
    build(nc, *args, out)
    result = run_bass_kernel_spmd(nc, [arrays], core_ids=[0])
    return result.results[0]["out"]
```

```python
from contextlib import ExitStack

import concourse.bass as bass
import concourse.mybir as mybir

F32 = mybir.dt.float32
F32R = mybir.dt.float32r
I32 = mybir.dt.int32
ALU = mybir.AluOpType
ACT = mybir.ActivationFunctionType
AX = mybir.AxisListType.X

B, N, D = 4, 256, 256
P = 128
H, HD = 32, 8
TPB = N // P
T = B * TPB
KD = D // P
HQ = 4
Q = H // HQ
STRIP = 32
E, I, TOP = 8, 512, 4
KI = I // P
HALF = B * N // 2
HT = HALF // P
LN_EPS, RMS_EPS = 1e-5, 1e-6
SCALE = float(HD) ** -0.5
MAGIC = float(0x5F3759DF)
NEWTON = 3
PREP_AT = (1, 3, 4, 5, 6)

W1C, W2C, W3C = KD * I, KI * I, KI * D
SPLIT = 512
C_USES = 5
XC0 = 5


class Links:

    def __init__(self, eng, sem):
        self.eng, self.sem, self.n = eng, sem, 0

    def mark(self, ins):
        ins.then_inc(self.sem, 1)
        self.n += 1
        return self.n

    def wait(self, value):
        self.eng.wait_ge(self.sem, value)

    def after(self, ins):
        self.wait(self.mark(ins))


def build(nc, x, ctx, Wq, Wk, Wv, rw, w1, w2, w3, out):
    es = ExitStack()

    def sb(name, cols, dt=F32):
        return es.enter_context(nc.sbuf_tensor(name, [P, *cols], dt))

    def sem(name):
        return es.enter_context(nc.semaphore(name))

    with es:
        ident = sb("ident", [P])
        x_sb = sb("x_sb", [T, D])
        ctx_sb = sb("ctx_sb", [TPB, D])
        w_raw = sb("w_raw", [3, TPB, D])
        wT_hi, wT_lo = sb("wT_hi", [3, KD, D], F32R), sb("wT_lo", [3, KD, D], F32R)
        rw_sb = sb("rw_sb", [KD, P])
        rw_hi, rw_lo = sb("rw_hi", [KD, P], F32R), sb("rw_lo", [KD, P], F32R)
        before = sb("before", [E, E])
        stats1, mv1 = sb("stats1", [T, 6]), sb("mv1", [T, 2])
        a1, y1, t1 = sb("a1", [T]), sb("y1", [T]), sb("t1", [T])
        stats2, mv2 = sb("stats2", [TPB, 6]), sb("mv2", [TPB, 2])
        a2, y2, t2 = sb("a2", [TPB]), sb("y2", [TPB]), sb("t2", [TPB])
        ssq = sb("ssq", [2, TPB * H])
        a3, y3, t3 = sb("a3", [2, TPB * H]), sb("y3", [2, TPB * H]), sb("t3", [2, TPB * H])
        xn = sb("xn", [TPB, D])
        xT_hi, xT_lo = sb("xT_hi", [KD, N], F32R), sb("xT_lo", [KD, N], F32R)
        cT_hi, cT_lo = sb("cT_hi", [KD, N], F32R), sb("cT_lo", [KD, N], F32R)
        q_sb = sb("q_sb", [TPB, D])
        kv_sb = sb("kv_sb", [TPB, 2 * D])
        tmp = sb("tmp", [2, TPB * D])
        big = [sb(f"big{i}", [4, I], F32R) for i in range(4)]
        qk_part = [big[i][:].rearrange("p a b -> p (a b)").rearrange("p (j x) -> p j x", j=TPB) for i in range(2)]
        qkT = [big[2 + i] for i in range(2)]
        v_ext = sb("v_ext", [TPB, H, STRIP])
        probs = sb("probs", [2, HQ, TPB * N])
        oT = sb("oT", [Q, N])
        r_den = sb("r_den", [4, H // 2])
        att = sb("att", [TPB, D])
        x2n = sb("x2n", [TPB, D])
        acc = sb("acc", [T, D])
        x2T_hi, x2T_lo = sb("x2T_hi", [KD, T * P], F32R), sb("x2T_lo", [KD, T * P], F32R)
        logT = sb("logT", [T * P])
        logits = sb("logits", [T, E])
        row = sb("row", [4, T])
        pr = sb("pr", [T, E])
        gt = sb("gt", [T * E, E])
        eq = sb("eq", [T * E, E])
        gates = sb("gates", [T, E])
        raw = sb("raw", [W1C + W2C + W3C])
        w_hi, w_lo = sb("w_hi", [W1C + W2C + W3C], F32R), sb("w_lo", [W1C + W2C + W3C], F32R)
        silu = probs[:, 0]
        h1_hi, h1_lo, h2_hi, h2_lo = big[0], big[1], big[2], big[3]

        s_bank = [es.enter_context(nc.psum_tensor(f"s_bank{i}", [P, 512], F32)) for i in range(4)]
        pv_bank = es.enter_context(nc.psum_tensor("pv_bank", [P, 512], F32))
        bank_a = es.enter_context(nc.psum_tensor("bank_a", [P, 512], F32))
        bank_b = es.enter_context(nc.psum_tensor("bank_b", [P, 512], F32))
        bank_c = es.enter_context(nc.psum_tensor("bank_c", [P, 512], F32))
        out_bank = [pv_bank, bank_a, bank_b, bank_c]

        x_in, x_rest_in, ctx_in, (wq_in, wk_in, wv_in), rw_in = sem("x_in"), sem("x_rest_in"), sem("ctx_in"), [sem("wq_in"), sem("wk_in"), sem("wv_in")], sem("rw_in")
        w_in = [sem("w1_in"), sem("w2_in"), sem("w3_in")]
        ident_ready, v_const_ready, mask_ready = sem("ident_ready"), sem("v_const_ready"), sem("mask_ready")
        pool_zeroed = sem("pool_zeroed")
        dve_step, pool_step, act_step = sem("dve_step"), sem("pool_step"), sem("act_step")
        a_full, pro_full, hi_copied, xc_ready, qkv_ready = sem("a_full"), sem("pro_full"), sem("hi_copied"), sem("xc_ready"), sem("qkv_ready")
        b_full, b_free = sem("b_full"), sem("b_free")
        c_full, c_free = sem("c_full"), sem("c_free")
        mv1_ready, rstd1_ready, xn_ready = sem("mv1_ready"), sem("rstd1_ready"), sem("xn_ready")
        ssq_ready, rrms_ready, parts_ready, v_ready = sem("ssq_ready"), sem("rrms_ready"), sem("parts_ready"), sem("v_ready")
        normed, hi_ready = sem("normed"), sem("hi_ready")
        s_full, exp_done, pv_done, pv_free = sem("s_full"), sem("exp_done"), sem("pv_done"), sem("pv_free")
        mv2_ready, rstd2_ready, x2n_ready, x2T_ready = sem("mv2_ready"), sem("rstd2_ready"), sem("x2n_ready"), sem("x2T_ready")
        rw_split, gates_ready, shifted, exped = sem("rw_split"), sem("gates_ready"), sem("shifted"), sem("exped")
        w_hi_ready, w_lo_ready = [sem(f"w{m}_hi_ready") for m in (1, 2, 3)], [sem(f"w{m}_lo_ready") for m in (1, 2, 3)]
        z_full, rw_zeroed = sem("z_full"), sem("rw_zeroed")
        silu_ready, h_hi_ready, h_ready = sem("silu_ready"), sem("h_hi_ready"), sem("h_ready")
        o_full, o_free, out_done = sem("o_full"), sem("o_free"), sem("out_done")
        block = es.enter_context(nc.Block())

        tmps = [tmp[:, s, :].rearrange("p (r d) -> p r d", d=HD) for s in range(2)]

        def twice(v):
            return v.unsqueeze(2).to_broadcast([P, TPB * H, 2, HD])

        def part(s, lo):
            v = qk_part[s].rearrange("p j (h x) -> p (j h) x", x=STRIP)
            if s == 0:
                return v.rearrange("p r (c s d) -> p r c s d", s=2, d=HD)[:, :, :, lo, :]
            return v.rearrange("p r (s c d) -> p r s c d", s=2, d=HD)[:, :, lo, :, :]

        def flat(v):
            return v[:].rearrange("p a b -> p (a b)")

        W_OFF = [0, W1C, W1C + W2C]
        W_COLS = [W1C, W2C, W3C]
        W_STEPS = [c // SPLIT for c in W_COLS]

        def parts_read(m, e):
            return ((z_full, 16 * e + 12), (z_full, 16 * e + 16), (o_full, T * (e + 1)))[m]

        @block.sync
        def _(sp):
            sp.dma_start(x_sb[:, 0:TPB, :], x[0].rearrange("(j p) d -> p j d", p=P)).then_inc(x_in, 16)
            sp.dma_start(w_raw[:, 1], Wk.rearrange("(o p) d -> p o d", p=P)).then_inc(wk_in, 16)
            sp.dma_start(w_raw[:, 2], Wv.rearrange("(o p) d -> p o d", p=P)).then_inc(wv_in, 16)
            sp.dma_start(w_raw[:, 0], Wq.rearrange("(o p) d -> p o d", p=P)).then_inc(wq_in, 16)
            sp.wait_ge(rw_zeroed, 1)
            sp.dma_start(rw_sb[:, :, 0:E], rw.rearrange("(k p) e -> p k e", p=P)).then_inc(rw_in, 16)

            def load_expert(e):
                for m, (w, k, width) in enumerate(((w1, KD, I), (w2, KI, I), (w3, KI, D))):
                    if not (isinstance(e, int) and e == 0):
                        sp.wait_ge(w_hi_ready[m], e * W_STEPS[m])
                        sp.wait_ge(w_lo_ready[m], e * W_STEPS[m])
                    src = w[bass.ds(e, 1)].rearrange("a (k p) n -> p (a k) n", p=P)
                    dst = raw[:, W_OFF[m]:W_OFF[m] + W_COLS[m]].rearrange("p (k n) -> p k n", n=width)
                    sp.dma_start(dst, src).then_inc(w_in[m], 16)

            load_expert(0)
            for b in range(1, B):
                if b == 1:
                    sp.wait_ge(pro_full, 3)
                else:
                    sp.wait_ge(a_full, 5 * (b - 2) + 1)
                sp.dma_start(ctx_sb[:], ctx[b].rearrange("(j p) d -> p j d", p=P)).then_inc(ctx_in, 16)
            with sp.Fori(1, E) as e:
                load_expert(e)
            for t in range(T):
                sp.wait_ge(o_free, (E - 1) * T + t + 1)
                sp.dma_start(out[t // TPB, (t % TPB) * P:(t % TPB + 1) * P, :], acc[:, t, :]).then_inc(out_done, 16)
            sp.wait_ge(out_done, 16 * T)

        @block.gpsimd
        def _(pool):
            links = Links(pool, pool_step)
            pool.memset(rw_sb[:], 0.0).then_inc(rw_zeroed, 1)
            pool.memset(ident[:], 0.0).then_inc(pool_zeroed, 1)
            pool.wait_ge(pool_zeroed, 1)
            pool.affine_select(out=ident[:], in_=ident[:], compare_op=ALU.not_equal, fill=1.0, base=0,
                               pattern=[[-1, P]], channel_multiplier=1).then_inc(ident_ready, 1)
            links.after(pool.memset(v_ext[:], 0.0))
            pool.memset(v_ext[:, :, :, HD:HD + 1], 1.0).then_inc(v_const_ready, 1)
            links.after(pool.memset(before[:], 0.0))
            for i in range(1, E):
                pool.memset(before[:, i, 0:i], 1.0).then_inc(mask_ready, 1)

            def rsqrt(a, y, t, src, mul, eps, done):
                links.after(pool.tensor_scalar(a, src, mul, eps, ALU.mult, ALU.add))
                links.after(pool.tensor_scalar(y.bitcast(I32), a.bitcast(I32), -0.5, MAGIC, ALU.mult, ALU.add))
                for n in range(NEWTON):
                    links.after(pool.tensor_tensor(t, y, y, ALU.mult))
                    links.after(pool.tensor_tensor(t, t, a, ALU.mult))
                    links.after(pool.tensor_scalar(t, t, -0.5, 1.5, ALU.mult, ALU.add))
                    last = pool.tensor_tensor(y, y, t, ALU.mult)
                    if n < NEWTON - 1:
                        links.after(last)
                last.then_inc(done, 1)

            def norm1(t0, t1_, done):
                pool.wait_ge(mv1_ready, t1_)
                rsqrt(a1[:, t0:t1_], y1[:, t0:t1_], t1[:, t0:t1_], mv1[:, t0:t1_, 1], 1.0, LN_EPS, done)

            def rms(b):
                pool.wait_ge(ssq_ready, 2 * b)
                rsqrt(a3[:], y3[:], t3[:], ssq[:], 1.0 / HD, RMS_EPS, rrms_ready)

            def round_qk(b):
                if b > 0:
                    pool.wait_ge(b_full, Q * b)
                for n, s in enumerate((1, 0)):
                    pool.wait_ge(normed, 2 * b + n + 1)
                    pool.tensor_scalar(part(s, 0), twice(tmps[s]), 1.0, 0.0, ALU.mult, ALU.add).then_inc(hi_ready, 1)

            def values(b):
                pool.wait_ge(qkv_ready, 3 * b + 2)
                if b == 0:
                    pool.wait_ge(v_const_ready, 1)
                else:
                    pool.wait_ge(pv_done, Q * b)
                for c in range(TPB):
                    v = kv_sb[:, c, :].rearrange("p (h d s) -> p h d s", d=HD, s=2)[:, :, :, 1]
                    pool.tensor_scalar(v_ext[:, c, :, 0:HD], v, 1.0, 0.0, ALU.mult, ALU.add).then_inc(v_ready, 1)

            def norm2(b):
                pool.wait_ge(mv2_ready, TPB * (b + 1))
                rsqrt(a2[:], y2[:], t2[:], mv2[:, :, 1], 1.0, LN_EPS, rstd2_ready)

            def split(m):
                pool.wait_ge(w_in[m], 16)
                for s in range(W_STEPS[m]):
                    cols = slice(W_OFF[m] + s * SPLIT, W_OFF[m] + (s + 1) * SPLIT)
                    pool.tensor_scalar(w_hi[:, cols], raw[:, cols], 1.0, 0.0, ALU.mult, ALU.add).then_inc(w_hi_ready[m], 1)

            norm1(0, TPB, rstd1_ready)
            round_qk(0)
            values(0)
            norm1(TPB, T, rstd1_ready)

            def step(b, first=False, last=False):
                if not last:
                    rms(b + 1)
                if not first:
                    norm2(b - 1)
                if not last:
                    round_qk(b + 1)
                    values(b + 1)

            step(0, first=True)
            for b in range(1, B):
                step(b, last=(b == B - 1))
            for m in range(3):
                split(m)
            norm2(B - 1)

        @block.scalar
        def _(act):
            act.dma_start(ctx_sb[:], ctx[0].rearrange("(j p) d -> p j d", p=P)).then_inc(ctx_in, 16)
            act.dma_start(x_sb[:, TPB:, :].rearrange("p (b j) d -> p b j d", j=TPB),
                          x[1:].rearrange("b (j p) d -> p b j d", p=P)).then_inc(x_rest_in, 16)

            def hi_copy(dst, bank, sem, value):
                act.wait_ge(sem, value)
                act.activation(dst, bank[:], ACT.Copy).then_inc(hi_copied, 1)

            def copy_a(b, use, dst):
                if use == 1:
                    act.wait_ge(normed, 2 * b)
                    act.wait_ge(v_ready, TPB * b)
                act.wait_ge(a_full, 5 * (b - 1) + use + 1)
                act.activation(dst, bank_a[:], ACT.Copy).then_inc(qkv_ready, 1)

            def copy_pv(b, g):
                act.wait_ge(pv_done, Q * b + g + 1)
                if b > 0 and g in (0, 4):
                    act.wait_ge(c_full, C_USES * (b - 1) + (2 if g == 0 else 4))
                act.activation(oT[:, g, :], pv_bank[:, 0:N], ACT.Copy).then_inc(pv_free, 1)

            def step(b, last):
                for h in range(2 * Q):
                    g, pair = h // 2, h % 2
                    if pair == 0 and not (b == 0 and g < 2):
                        act.wait_ge(pv_done, Q * b + g - 1)
                    for r in (2 * pair, 2 * pair + 1):
                        act.wait_ge(s_full, HQ * (Q * b + g) + r + 1)
                        act.activation(probs[:, g % 2, r, :], s_bank[r][:], ACT.Exp, scale=SCALE).then_inc(exp_done, 1)
                    if pair == 1 and g > 0:
                        copy_pv(b, g - 1)
                    if not last:
                        if h == 1:
                            hi_copy(flat(cT_hi), bank_a, a_full, 5 * b + 1)
                        if h in (3, 4):
                            copy_a(b + 1, h - 2, kv_sb[:, h - 3, :])
                        if h == 5:
                            hi_copy(flat(xT_hi), bank_a, a_full, 5 * b + 4)
                        if h == 6:
                            copy_a(b + 1, 4, flat(q_sb))
                copy_pv(b, Q - 1)

            for n, (dst, bank) in enumerate(((flat(wT_hi[:, 1]), s_bank[0]), (flat(wT_hi[:, 2]), s_bank[1]), (flat(cT_hi), bank_b))):
                hi_copy(dst, bank, pro_full, n + 1)
            for c, bank in enumerate((s_bank[3], pv_bank)):
                act.wait_ge(pro_full, 4 + c)
                act.activation(kv_sb[:, c, :], bank[:], ACT.Copy).then_inc(qkv_ready, 1)
            for n, (dst, bank) in enumerate(((flat(wT_hi[:, 0]), s_bank[2]), (flat(xT_hi), bank_a))):
                hi_copy(dst, bank, pro_full, n + 6)
            act.wait_ge(pro_full, 8)
            act.activation(flat(q_sb), bank_c[:], ACT.Copy).then_inc(qkv_ready, 1)
            for b in range(B):
                step(b, b == B - 1)

            def hidden(first, hi):
                for m in range(KI):
                    act.wait_ge(z_full, first + m + 1)
                    if not (isinstance(first, int) and first == 0):
                        act.wait_ge(h_ready, first + m - 3)
                    act.activation(silu[:, m, :], s_bank[m][:], ACT.Silu).then_inc(silu_ready, 1)
                    act.activation(hi[:, m, :], s_bank[m][:], ACT.Silu).then_inc(h_hi_ready, 1)

            def split(m, e):
                act.wait_ge(w_in[m], 16 * (e + 1))
                act.wait_ge(*parts_read(m, e - 1))
                for s in range(W_STEPS[m]):
                    cols = slice(W_OFF[m] + s * SPLIT, W_OFF[m] + (s + 1) * SPLIT)
                    act.activation(w_hi[:, cols], raw[:, cols], ACT.Copy).then_inc(w_hi_ready[m], 1)

            def expert(e, first=False, last=False):
                hidden(16 * e + 4, h2_hi)
                hidden(16 * e + 8, h1_hi)
                if first:
                    act.wait_ge(shifted, 1)
                    act.activation(pr[:], pr[:], ACT.Exp).then_inc(exped, 1)
                if not last:
                    split(0, e + 1)
                hidden(16 * e + 12, h2_hi)
                if not last:
                    hidden(16 * e + 16, h1_hi)
                    split(1, e + 1)
                    split(2, e + 1)

            hidden(0, h1_hi)
            expert(0, first=True)
            with act.Fori(1, E - 1) as e:
                expert(e)
            expert(E - 1, last=True)

        @block.vector
        def _(dve):
            links = Links(dve, dve_step)

            def lo_copy(dst, bank, hi, n):
                dve.wait_ge(hi_copied, n + 1)
                dve.tensor_tensor(dst, bank[:], hi.bitcast(F32), ALU.subtract).then_inc(xc_ready, 1)

            def x_norm(b):
                if b == 1:
                    dve.wait_ge(rstd1_ready, 2)
                for j in range(TPB):
                    t = TPB * b + j
                    dve.tensor_scalar(xn[:, j, :], x_sb[:, t, :],
                                      mv1[:, t, 0:1], y1[:, t:t + 1],
                                      ALU.subtract, ALU.mult).then_inc(xn_ready, 1)

            q_in = q_sb[:].rearrange("p j (h d) -> p (j h) d", d=HD)
            k_in = kv_sb[:].rearrange("p c (h d s) -> p (c h) d s", d=HD, s=2)[:, :, :, 0]

            def squares(b, s, done=None):
                dve.wait_ge(qkv_ready, 3 * b + (3 if s == 0 else 2))
                v = (q_in, k_in)[s]
                links.after(dve.tensor_tensor(tmps[s], v, v, ALU.mult))
                done(dve.tensor_reduce(ssq[:, s, :], tmps[s], AX, ALU.add))

            def rms0(s):
                squares(0, s, links.after)
                a, y, t = a3[:, s, :], y3[:, s, :], t3[:, s, :]
                links.after(dve.tensor_scalar(a, ssq[:, s, :], 1.0 / HD, RMS_EPS, ALU.mult, ALU.add))
                links.after(dve.tensor_scalar(y.bitcast(I32), a.bitcast(I32), -0.5, MAGIC, ALU.mult, ALU.add))
                for n in range(NEWTON):
                    links.after(dve.tensor_tensor(t, y, y, ALU.mult))
                    links.after(dve.scalar_tensor_tensor(t, t, -0.5, a, ALU.mult, ALU.mult))
                    links.after(dve.scalar_tensor_tensor(y, t, 1.5, y, ALU.add, ALU.mult))
                normalize(s)

            def normalize(s):
                r = y3[:, s, :].unsqueeze(2).to_broadcast([P, TPB * H, HD])
                dve.tensor_tensor(tmps[s], (q_in, k_in)[s], r, ALU.mult).then_inc(normed, 1)

            def part_lo(b, n):
                s = 1 - n
                dve.wait_ge(hi_ready, 2 * b + n + 1)
                dve.tensor_tensor(part(s, 1), twice(tmps[s]), part(s, 0).bitcast(F32), ALU.subtract).then_inc(parts_ready, 1)

            def evac_b(b, g):
                dve.wait_ge(b_full, Q * b + g + 1)
                if b > 0:
                    dve.wait_ge(s_full, HQ * (Q * (b - 1) + g + 1))
                dve.tensor_copy(qkT[g // 4][:, g % 4, :], bank_b[:]).then_inc(b_free, 1)

            def divide(b, half, j):
                use = 2 * half + j
                dve.wait_ge(c_full, C_USES * b + use + 1)
                o = bank_c[:].rearrange("p (h s) -> p h s", s=STRIP)
                links.after(dve.reciprocal(r_den[:, use, :], o[:, :, HD]))
                dst = att[:, j, half * P:(half + 1) * P].rearrange("p (h d) -> p h d", d=HD)
                den = r_den[:, use, :].unsqueeze(2).to_broadcast([P, H // 2, HD])
                dve.tensor_tensor(dst, o[:, :, 0:HD], den, ALU.mult).then_inc(c_free, 1)

            def residual(b):
                dve.wait_ge(c_free, C_USES * b + 4)
                tiles = slice(TPB * b, TPB * (b + 1))
                done = links.mark(dve.tensor_tensor(acc[:, tiles, :], att[:], x_sb[:, tiles, :], ALU.add))
                links.wait(done)
                for j in range(TPB):
                    done = links.mark(dve.bn_stats(stats2[:, j, :], acc[:, TPB * b + j, :]))
                links.wait(done)
                for j in range(TPB):
                    dve.bn_aggr(mv2[:, j, :], stats2[:, j, :]).then_inc(mv2_ready, 1)

            def x2_norm(b):
                dve.wait_ge(rstd2_ready, b + 1)
                for j in range(TPB):
                    dve.tensor_scalar(x2n[:, j, :], acc[:, TPB * b + j, :],
                                      mv2[:, j, 0:1], y2[:, j:j + 1], ALU.subtract, ALU.mult).then_inc(x2n_ready, 1)

            def x2_parts(b):
                dve.wait_ge(c_full, C_USES * b + 5)
                cols = slice(N * b, N * (b + 1))
                full = bank_c[:].rearrange("p (k n) -> p k n", k=KD)
                links.after(dve.tensor_copy(x2T_hi[:, :, cols], full))
                dve.tensor_tensor(x2T_lo[:, :, cols], full, x2T_hi[:, :, cols].bitcast(F32), ALU.subtract).then_inc(c_free, 1)

            def split(m, e):
                dve.wait_ge(w_in[m], 16 * (e + 1))
                if not (isinstance(e, int) and e == 0):
                    dve.wait_ge(*parts_read(m, e - 1))
                for s in range(W_STEPS[m]):
                    cols = slice(W_OFF[m] + s * SPLIT, W_OFF[m] + (s + 1) * SPLIT)
                    dve.wait_ge(w_hi_ready[m], W_STEPS[m] * e + s + 1)
                    dve.tensor_tensor(w_lo[:, cols], raw[:, cols], w_hi[:, cols].bitcast(F32),
                                      ALU.subtract).then_inc(w_lo_ready[m], 1)

            def step(b, first=False, last=False):
                for h in range(2 * Q):
                    if h % 2 == 0 and h // 2 < Q - 1:
                        evac_b(b, h // 2 + 1)
                    if not first:
                        if h < 4:
                            divide(b - 1, h // 2, h % 2)
                        if h == 3:
                            residual(b - 1)
                        if h == 9:
                            x2_norm(b - 1)
                        if h == 11:
                            x2_parts(b - 1)
                    if last:
                        if h in (8, 9, 10):
                            split(h - 8, 0)
                        if h in (13, 14):
                            divide(b, 0, h - 13)
                        continue
                    if h == 1:
                        lo_copy(flat(cT_lo), bank_a, flat(cT_hi), XC0 + 2 * b)
                    if h == 4:
                        x_norm(b + 1)
                    if h == 5:
                        squares(b + 1, 1, lambda i: i.then_inc(ssq_ready, 1))
                        lo_copy(flat(xT_lo), bank_a, flat(xT_hi), XC0 + 2 * b + 1)
                    if h == 7:
                        squares(b + 1, 0, lambda i: i.then_inc(ssq_ready, 1))
                    if h == 13:
                        dve.wait_ge(rrms_ready, b + 1)
                        normalize(1)
                        normalize(0)
                    if h == 15:
                        part_lo(b + 1, 0)
                        part_lo(b + 1, 1)
                if not last:
                    evac_b(b + 1, 0)

            def stats(t0, t1_):
                dve.wait_ge(x_in if t0 == 0 else x_rest_in, 16)
                for t in range(t0, t1_):
                    done = links.mark(dve.bn_stats(stats1[:, t, :], x_sb[:, t, :]))
                links.wait(done)
                for t in range(t0, t1_):
                    dve.bn_aggr(mv1[:, t, :], stats1[:, t, :]).then_inc(mv1_ready, 1)

            stats(0, TPB)
            lo_copy(flat(wT_lo[:, 1]), s_bank[0], flat(wT_hi[:, 1]), 0)
            lo_copy(flat(wT_lo[:, 2]), s_bank[1], flat(wT_hi[:, 2]), 1)
            lo_copy(flat(cT_lo), bank_b, flat(cT_hi), 2)
            dve.wait_ge(rstd1_ready, 1)
            x_norm(0)
            rms0(1)
            lo_copy(flat(wT_lo[:, 0]), s_bank[2], flat(wT_hi[:, 0]), 3)
            lo_copy(flat(xT_lo), bank_a, flat(xT_hi), 4)
            part_lo(0, 0)
            rms0(0)
            part_lo(0, 1)
            evac_b(0, 0)
            stats(TPB, T)
            dve.wait_ge(rw_in, 16)
            links.after(dve.tensor_copy(rw_hi[:], rw_sb[:]))
            dve.tensor_tensor(rw_lo[:], rw_sb[:], rw_hi[:].bitcast(F32), ALU.subtract).then_inc(rw_split, 1)

            step(0, first=True)
            for b in range(1, B):
                step(b, last=(b == B - 1))

            def hidden(first, hi, lo, chunks=range(KI)):
                for m in chunks:
                    dve.wait_ge(silu_ready, first + m + 1)
                    dve.wait_ge(h_hi_ready, first + m + 1)
                    dve.tensor_tensor(lo[:, m, :], silu[:, m, :], hi[:, m, :].bitcast(F32), ALU.subtract).then_inc(h_ready, 1)

            def combine(e, t):
                for j in range(HT):
                    tile = HT * t + j
                    dve.wait_ge(o_full, T * e + tile + 1)
                    dve.scalar_tensor_tensor(acc[:, tile, :], out_bank[j][:, 0:D], gates[:, tile, bass.ds(e, 1)],
                                             acc[:, tile, :], ALU.mult, ALU.add).then_inc(o_free, 1)

            def expert(e, first=False, last=False):
                if first:
                    hidden(4, h2_hi, h2_lo, range(1))
                    x2_parts(B - 1)
                    hidden(4, h2_hi, h2_lo, range(1, KI))
                else:
                    hidden(16 * e + 4, h2_hi, h2_lo)
                hidden(16 * e + 8, h1_hi, h1_lo)
                if first:
                    router()
                if not last:
                    split(0, e + 1)
                combine(e, 0)
                hidden(16 * e + 12, h2_hi, h2_lo)
                if not last:
                    hidden(16 * e + 16, h1_hi, h1_lo)
                    split(1, e + 1)
                combine(e, 1)
                if not last:
                    split(2, e + 1)

            def router():
                le = [P, T, E]
                for half in range(2):
                    dve.wait_ge(c_full, C_USES * B + half + 1)
                    dve.tensor_copy(logT[0:E, half * HALF:(half + 1) * HALF], bank_c[0:E, :]).then_inc(c_free, 1)
                dve.wait_ge(c_full, C_USES * B + 3)
                dve.tensor_copy(flat(logits), bank_c[:, 0:T * E]).then_inc(c_free, 1)
                dve.wait_ge(c_free, C_USES * B + 3)
                links.after(dve.tensor_reduce(row[:, 0, :], logits[:], AX, ALU.max))
                dve.tensor_tensor(pr[:], logits[:], row[:, 0, :].unsqueeze(2).to_broadcast(le), ALU.subtract).then_inc(shifted, 1)
                dve.wait_ge(exped, 1)
                links.after(dve.tensor_reduce(row[:, 1, :], pr[:], AX, ALU.add))
                links.after(dve.reciprocal(row[:, 2, :], row[:, 1, :]))
                links.after(dve.tensor_tensor(pr[:], pr[:], row[:, 2, :].unsqueeze(2).to_broadcast(le), ALU.mult))
                other = pr[:].unsqueeze(2).to_broadcast([P, T, E, E])
                own = pr[:].unsqueeze(3).to_broadcast([P, T, E, E])
                v4 = lambda m: m[:].rearrange("p (t i) j -> p t i j", i=E)
                links.mark(dve.tensor_tensor(v4(gt), other, own, ALU.is_gt))
                links.after(dve.tensor_tensor(v4(eq), other, own, ALU.is_equal))
                dve.wait_ge(mask_ready, E - 1)
                links.after(dve.tensor_tensor(v4(eq), v4(eq), before[:].unsqueeze(1).to_broadcast([P, T, E, E]), ALU.mult))
                links.after(dve.tensor_tensor(gt[:], gt[:], eq[:], ALU.add))
                g = flat(gates)
                links.after(dve.tensor_reduce(g, gt[:], AX, ALU.add))
                links.after(dve.tensor_scalar(g, g, float(TOP), None, ALU.is_lt))
                links.after(dve.tensor_tensor(pr[:], pr[:], gates[:], ALU.mult))
                links.after(dve.tensor_reduce(row[:, 3, :], pr[:], AX, ALU.add))
                links.after(dve.reciprocal(row[:, 1, :], row[:, 3, :]))
                links.after(dve.tensor_tensor(gates[:], pr[:], row[:, 1, :].unsqueeze(2).to_broadcast(le), ALU.mult))

            divide(B - 1, 1, 0)
            divide(B - 1, 1, 1)
            residual(B - 1)
            hidden(0, h1_hi, h1_lo)
            x2_norm(B - 1)
            expert(0, first=True)
            with dve.Fori(1, E - 1) as e:
                expert(e)
            expert(E - 1, last=True)

        @block.tensor
        def _(pe):
            def transpose(bank, src):
                for j in range(TPB):
                    for c in range(KD):
                        last = pe.transpose(bank[:, c * N + j * P:c * N + (j + 1) * P], src[:, j, c * P:(c + 1) * P], ident[:])
                return last

            def project(bank_cols, hi, lo, tok, w0, w1_):
                for k in range(KD):
                    for i, (v, w) in enumerate(((hi, wT_hi), (hi, wT_lo), (lo, wT_hi))):
                        last = pe.matmul(bank_cols, v[:, k, tok], w[:, w0:w1_, k, :], start=(k == 0 and i == 0),
                                         stop=(k == KD - 1 and i == 2))
                return last

            def project_kv(bank, c):
                return project(bank[:], cT_hi, cT_lo, slice(c * P, (c + 1) * P), 1, 3)

            def project_q(bank):
                for j in range(TPB):
                    last = project(bank[:, j * D:(j + 1) * D], xT_hi, xT_lo, slice(j * P, (j + 1) * P), 0, 1)
                return last

            def prep(b, use):
                if use == 0:
                    pe.wait_ge(qkv_ready, 3 * b)
                    pe.wait_ge(ctx_in, 16 * (b + 1))
                    last = transpose(bank_a, ctx_sb)
                elif use in (1, 2):
                    if use == 1:
                        pe.wait_ge(xc_ready, XC0 + 2 * b - 1)
                    else:
                        pe.wait_ge(qkv_ready, 3 * b + 1)
                    last = project_kv(bank_a, use - 1)
                elif use == 3:
                    pe.wait_ge(qkv_ready, 3 * b + 2)
                    pe.wait_ge(xn_ready, TPB * (b + 1))
                    last = transpose(bank_a, xn)
                else:
                    pe.wait_ge(xc_ready, XC0 + 2 * b)
                    last = project_q(bank_a)
                last.then_inc(a_full, 1)

            def qk_transpose(b, g):
                if g == 0:
                    pe.wait_ge(parts_ready, 2 * (b + 1))
                if not (b == 0 and g == 0):
                    pe.wait_ge(b_free, Q * b + g)
                for s in range(2):
                    for j in range(TPB):
                        v = qk_part[s][:, j, g * P:(g + 1) * P].bitcast(F32)
                        last = pe.transpose(bank_b[:, s * N + j * P:s * N + (j + 1) * P], v, ident[:])
                last.then_inc(b_full, 1)

            def scores(b, g, pair):
                if pair == 0:
                    pe.wait_ge(b_free, Q * b + g + 1)
                for c in range(TPB):
                    for r in (2 * pair, 2 * pair + 1):
                        if c == 0 and not (b == 0 and g == 0):
                            pe.wait_ge(exp_done, HQ * (Q * b + g - 1) + r + 1)
                        rows = slice(STRIP * r, STRIP * (r + 1))
                        qk = qkT[g // 4][rows, g % 4, :]
                        last = pe.matmul(s_bank[r][:, c * N:(c + 1) * N], qk[:, N + c * P:N + (c + 1) * P], qk[:, 0:N],
                                         start=True, stop=True)
                        if c == TPB - 1:
                            last.then_inc(s_full, 1)

            def values(b, g, c):
                if c == 0:
                    if g == 0:
                        pe.wait_ge(v_ready, TPB * (b + 1))
                    if not (b == 0 and g == 0):
                        pe.wait_ge(pv_free, Q * b + g)
                    pe.wait_ge(exp_done, HQ * (Q * b + g + 1))
                for r in range(HQ):
                    rows = slice(STRIP * r, STRIP * (r + 1))
                    last = pe.matmul(pv_bank[rows, 0:N], v_ext[:, c, HQ * g + r, :], probs[:, g % 2, r, c * N:(c + 1) * N],
                                     start=(c == 0), stop=(c == TPB - 1), tile_position=(0, STRIP * r))
                if c == TPB - 1:
                    last.then_inc(pv_done, 1)

            def before_c(u):
                if u > 0:
                    pe.wait_ge(c_free, u)

            def o_transpose(b, half, j):
                before_c(C_USES * b + 2 * half + j)
                pe.wait_ge(pv_free, Q * b + 4 * (half + 1))
                for g in range(4):
                    last = pe.transpose(bank_c[:, g * P:(g + 1) * P], oT[:, 4 * half + g, j * P:(j + 1) * P], ident[:])
                last.then_inc(c_full, 1)

            def x2_transpose(b):
                pe.wait_ge(x2n_ready, TPB * (b + 1))
                before_c(C_USES * b + 4)
                for j in range(TPB):
                    for k in range(KD):
                        last = pe.transpose(bank_c[:, k * N + j * P:k * N + (j + 1) * P], x2n[:, j, k * P:(k + 1) * P], ident[:])
                last.then_inc(c_full, 1)

            def step(b, first=False, last=False):
                for h in range(2 * Q):
                    g, pair = h // 2, h % 2
                    scores(b, g, pair)
                    if pair == 0 and g < Q - 1:
                        qk_transpose(b, g + 1)
                    if g > 0:
                        values(b, g - 1, pair)
                    if not first and h < 4:
                        o_transpose(b - 1, h // 2, h % 2)
                    if not first and h == 11:
                        x2_transpose(b - 1)
                    if last and h in (13, 14):
                        o_transpose(b, 0, h - 13)
                    if not last and h in PREP_AT:
                        prep(b + 1, PREP_AT.index(h))
                values(b, Q - 1, 0)
                values(b, Q - 1, 1)
                if not last:
                    qk_transpose(b + 1, 0)

            pe.wait_ge(ident_ready, 1)
            for m, bank, arrived in ((1, s_bank[0], wk_in), (2, s_bank[1], wv_in)):
                pe.wait_ge(arrived, 16)
                transpose(bank, w_raw[:, m]).then_inc(pro_full, 1)
            pe.wait_ge(ctx_in, 16)
            transpose(bank_b, ctx_sb).then_inc(pro_full, 1)
            pe.wait_ge(xc_ready, 3)
            project_kv(s_bank[3], 0).then_inc(pro_full, 1)
            project_kv(pv_bank, 1).then_inc(pro_full, 1)
            pe.wait_ge(wq_in, 16)
            transpose(s_bank[2], w_raw[:, 0]).then_inc(pro_full, 1)
            pe.wait_ge(xn_ready, TPB)
            transpose(bank_a, xn).then_inc(pro_full, 1)
            pe.wait_ge(xc_ready, XC0)
            project_q(bank_c).then_inc(pro_full, 1)
            qk_transpose(0, 0)
            step(0, first=True)
            for b in range(1, B):
                step(b, last=(b == B - 1))

            def weights(m, k, width, first, cols):
                at = slice(W_OFF[m] + k * width + first, W_OFF[m] + k * width + first + cols)
                return w_hi[:, at], w_lo[:, at]

            def layer(m, e, t, chunk, rhs_hi, rhs_lo, ks, cols, chunks=range(KI)):
                for n in chunks:
                    if not (isinstance(chunk, int) and chunk == 0):
                        pe.wait_ge(h_hi_ready, chunk + n - 3)
                    for k in range(ks):
                        if m == 1 and n == 0:
                            pe.wait_ge(h_ready, chunk + k - 3)
                        hi, lo = weights(m, k, I, n * P, P)
                        for i, (w, r) in enumerate(((hi, rhs_hi), (hi, rhs_lo), (lo, rhs_hi))):
                            last = pe.matmul(s_bank[n][:], w, r[:, k, cols], start=(k == 0 and i == 0),
                                             stop=(k == ks - 1 and i == 2))
                    last.then_inc(z_full, 1)

            def layer1(e, t):
                if t == 0:
                    pe.wait_ge(w_lo_ready[0], W_STEPS[0] * (e + 1))
                layer(0, e, t, 16 * e + 8 * t, x2T_hi, x2T_lo, KD, slice(t * HALF, (t + 1) * HALF))

            def layer2(e, t, chunks=range(KI)):
                if t == 0 and 0 in chunks:
                    pe.wait_ge(w_lo_ready[1], W_STEPS[1] * (e + 1))
                layer(1, e, t, 16 * e + 8 * t + 4, h1_hi, h1_lo, KI, slice(0, HALF), chunks)

            def layer3(e, t):
                if t == 0:
                    pe.wait_ge(w_lo_ready[2], W_STEPS[2] * (e + 1))
                for j in range(HT):
                    n = T * e + HT * t + j
                    if not (isinstance(n, int) and n < HT):
                        pe.wait_ge(o_free, n - HT + 1)
                    for k in range(KI):
                        if j == 0:
                            pe.wait_ge(h_ready, 16 * e + 8 * t + 4 + k + 1)
                        whi, wlo = weights(2, k, D, 0, D)
                        tok = slice(j * P, (j + 1) * P)
                        for i, (h, w) in enumerate(((h2_hi, whi), (h2_hi, wlo), (h2_lo, whi))):
                            last = pe.matmul(out_bank[j][:, 0:D], h[:, k, tok], w, start=(k == 0 and i == 0),
                                             stop=(k == KI - 1 and i == 2))
                    last.then_inc(o_full, 1)

            def router():
                pe.wait_ge(rw_split, 1)
                for half in range(2):
                    before_c(C_USES * B + half)
                    for k in range(KD):
                        for i, (w, r) in enumerate(((rw_hi, x2T_hi), (rw_hi, x2T_lo), (rw_lo, x2T_hi))):
                            last = pe.matmul(bank_c[:], w[:, k, :], r[:, k, half * HALF:(half + 1) * HALF],
                                             start=(k == 0 and i == 0), stop=(k == KD - 1 and i == 2))
                    last.then_inc(c_full, 1)
                before_c(C_USES * B + 2)
                for t in range(T):
                    last = pe.transpose(bank_c[:, t * E:(t + 1) * E], logT[0:E, t * P:(t + 1) * P], ident[0:E, 0:E])
                last.then_inc(c_full, 1)

            def expert(e, first=False, last=False):
                if first:
                    layer2(e, 0, range(2))
                    x2_transpose(B - 1)
                    layer2(e, 0, range(2, KI))
                    before_c(C_USES * B)
                else:
                    layer2(e, 0)
                layer1(e, 1)
                if first:
                    router()
                    before_c(C_USES * B + 3)
                layer3(e, 0)
                layer2(e, 1)
                if not last:
                    layer1(e + 1, 0)
                layer3(e, 1)

            o_transpose(B - 1, 1, 0)
            o_transpose(B - 1, 1, 1)
            layer1(0, 0)
            expert(0, first=True)
            with pe.Fori(1, E - 1) as e:
                expert(e)
            expert(E - 1, last=True)


_INS = ['x', 'ctx_2048', 'L0_xattn_Wq', 'L0_xattn_Wk', 'L0_xattn_Wv', 'L0_ffn_router_w', 'L0_ffn_w1', 'L0_ffn_w2', 'L0_ffn_w3']


def kernel(**inputs):
    import numpy as np
    import concourse.bacc as bacc
    from concourse.bass_utils import run_bass_kernel_spmd

    nc = bacc.Bacc("TRN2", target_bir_lowering=False, num_devices=1)
    arrays, args = {}, []
    for name in _INS:
        a = np.ascontiguousarray(inputs[name])
        arrays[f"in_{name}"] = a
        args.append(nc.dram_tensor(f"in_{name}", a.shape, mybir.dt.from_np(a.dtype), kind="ExternalInput").ap())
    out = nc.dram_tensor("out", (B, N, D), F32, kind="ExternalOutput").ap()
    build(nc, *args, out)
    result = run_bass_kernel_spmd(nc, [arrays], core_ids=[0])
    return result.results[0]["out"]
```

```python
from contextlib import ExitStack

import concourse.bass as bass
import concourse.mybir as mybir

F32 = mybir.dt.float32
F32R = mybir.dt.float32r
I32 = mybir.dt.int32
ALU = mybir.AluOpType
ACT = mybir.ActivationFunctionType
AX = mybir.AxisListType.X

B, N, D = 4, 256, 256
P = 128
H, HD = 32, 8
TPB = N // P
T = B * TPB
KD = D // P
HQ = 4
Q = H // HQ
STRIP = 32
E, I, TOP = 8, 512, 4
KI = I // P
HALF = B * N // 2
HT = HALF // P
LN_EPS, RMS_EPS = 1e-5, 1e-6
SCALE = float(HD) ** -0.5
MAGIC = float(0x5F3759DF)
NEWTON = 3
PREP_AT = (0, 1, 2, 4, 5)
QK_AT = (0, 2, 3, 5, 6, 7, 8)
O_AT = (0, 1, 3, 4)
WARM = 14

W1C, W2C, W3C = KD * I, KI * I, KI * D
SPLIT = 512
C_USES = 5
NORMS0 = 4
XC0 = 5
V_PARTS = 2 * TPB


class Links:

    def __init__(self, eng, sem):
        self.eng, self.sem, self.n = eng, sem, 0

    def mark(self, ins):
        ins.then_inc(self.sem, 1)
        self.n += 1
        return self.n

    def wait(self, value):
        self.eng.wait_ge(self.sem, value)

    def after(self, ins):
        self.wait(self.mark(ins))


def build(nc, x, ctx, Wq, Wk, Wv, rw, w1, w2, w3, out):
    es = ExitStack()

    def sb(name, cols, dt=F32):
        return es.enter_context(nc.sbuf_tensor(name, [P, *cols], dt))

    def sem(name):
        return es.enter_context(nc.semaphore(name))

    with es:
        ident = sb("ident", [P])
        x_sb = sb("x_sb", [T, D])
        ctx_sb = sb("ctx_sb", [TPB, D])
        w_raw = sb("w_raw", [3, TPB, D])
        wT_hi, wT_lo = sb("wT_hi", [3, KD, D], F32R), sb("wT_lo", [3, KD, D], F32R)
        rw_sb = sb("rw_sb", [KD, P])
        rw_hi, rw_lo = sb("rw_hi", [KD, P], F32R), sb("rw_lo", [KD, P], F32R)
        before = sb("before", [E, E])
        stats1, mv1 = sb("stats1", [T, 6]), sb("mv1", [T, 2])
        a1, y1, t1 = sb("a1", [T]), sb("y1", [T]), sb("t1", [T])
        stats2, mv2 = sb("stats2", [TPB, 6]), sb("mv2", [TPB, 2])
        a2, y2, t2 = sb("a2", [TPB]), sb("y2", [TPB]), sb("t2", [TPB])
        ssq = sb("ssq", [2, TPB * H])
        a3, y3, t3 = sb("a3", [2, TPB * H]), sb("y3", [2, TPB * H]), sb("t3", [2, TPB * H])
        xn = sb("xn", [TPB, D])
        xT_hi, xT_lo = sb("xT_hi", [KD, N], F32R), sb("xT_lo", [KD, N], F32R)
        cT_hi, cT_lo = sb("cT_hi", [KD, N], F32R), sb("cT_lo", [KD, N], F32R)
        q_sb = sb("q_sb", [TPB, D])
        kv_sb = sb("kv_sb", [TPB, 2 * D])
        tmp = sb("tmp", [2, TPB * D])
        big = [sb(f"big{i}", [4, I], F32R) for i in range(4)]
        qk_part = [big[i][:].rearrange("p a b -> p (a b)") for i in range(2)]
        qkT = [big[2 + i] for i in range(2)]
        v_ext = sb("v_ext", [TPB, H, STRIP])
        probs = sb("probs", [2, HQ, TPB * N])
        oT = sb("oT", [Q, N])
        r_den = sb("r_den", [4, H // 2])
        att = sb("att", [TPB, D])
        x2n = sb("x2n", [TPB, D])
        acc = sb("acc", [T, D])
        x2T_hi, x2T_lo = sb("x2T_hi", [KD, T * P], F32R), sb("x2T_lo", [KD, T * P], F32R)
        logT = sb("logT", [T * P])
        logits = sb("logits", [T, E])
        row = sb("row", [4, T])
        pr = sb("pr", [T, E])
        gt = sb("gt", [T * E, E])
        eq = sb("eq", [T * E, E])
        gates = sb("gates", [T, E])
        raw = sb("raw", [W1C + W2C + W3C])
        w_hi, w_lo = sb("w_hi", [W1C + W2C + W3C], F32R), sb("w_lo", [W1C + W2C + W3C], F32R)
        silu = probs[:, 0]
        h1_hi, h1_lo, h2_hi, h2_lo = big[0], big[1], big[2], big[3]

        s_bank = [es.enter_context(nc.psum_tensor(f"s_bank{i}", [P, 512], F32)) for i in range(4)]
        pv_bank = es.enter_context(nc.psum_tensor("pv_bank", [P, 512], F32))
        bank_a = es.enter_context(nc.psum_tensor("bank_a", [P, 512], F32))
        bank_b = es.enter_context(nc.psum_tensor("bank_b", [P, 512], F32))
        bank_c = es.enter_context(nc.psum_tensor("bank_c", [P, 512], F32))
        out_bank = [pv_bank, bank_a, bank_b, bank_c]

        x_in, x_rest_in, ctx_in, (wq_in, wk_in, wv_in), rw_in = sem("x_in"), sem("x_rest_in"), sem("ctx_in"), [sem("wq_in"), sem("wk_in"), sem("wv_in")], sem("rw_in")
        w_in = [sem("w1_in"), sem("w2_in"), sem("w3_in")]
        ident_ready, v_const_ready, mask_ready = sem("ident_ready"), sem("v_const_ready"), sem("mask_ready")
        pool_zeroed = sem("pool_zeroed")
        dve_step, pool_step, act_step = sem("dve_step"), sem("pool_step"), sem("act_step")
        a_full, pro_full, hi_copied, xc_ready, qkv_ready = sem("a_full"), sem("pro_full"), sem("hi_copied"), sem("xc_ready"), sem("qkv_ready")
        b_full, b_free = sem("b_full"), sem("b_free")
        c_full, c_free = sem("c_full"), sem("c_free")
        mv1_ready, rstd1_ready, xn_ready = sem("mv1_ready"), sem("rstd1_ready"), sem("xn_ready")
        parts_ready, v_ready = sem("parts_ready"), sem("v_ready")
        normed, hi_ready, k_hi_ready, q_hi_ready = sem("normed"), sem("hi_ready"), sem("k_hi_ready"), sem("q_hi_ready")
        s_full, exp_done, pv_done, pv_free = sem("s_full"), sem("exp_done"), sem("pv_done"), sem("pv_free")
        mv2_ready, rstd2_ready, x2n_ready, x2T_ready = sem("mv2_ready"), sem("rstd2_ready"), sem("x2n_ready"), sem("x2T_ready")
        rw_split, gates_ready, shifted, exped = sem("rw_split"), sem("gates_ready"), sem("shifted"), sem("exped")
        w_hi_ready, w_lo_ready = [sem(f"w{m}_hi_ready") for m in (1, 2, 3)], [sem(f"w{m}_lo_ready") for m in (1, 2, 3)]
        z_full, rw_zeroed = sem("z_full"), sem("rw_zeroed")
        silu_ready, h_hi_ready, h_ready = sem("silu_ready"), sem("h_hi_ready"), sem("h_ready")
        o_full, o_free, out_done = sem("o_full"), sem("o_free"), sem("out_done")
        block = es.enter_context(nc.Block())

        QH = TPB * HQ
        ALL, FRONT, BACK = (0, Q), (0, Q // 2), (Q // 2, Q)

        def rows_of(v, quads):
            return v.rearrange("p (r d) -> p r d", d=HD)[:, quads[0] * QH:quads[1] * QH, :]

        def twice(s, quads):
            v = rows_of(tmp[:, s, :], quads)
            return v.unsqueeze(2).to_broadcast([P, v.shape[1], 2, HD])

        def part(s, lo, quads):
            v = qk_part[s].rearrange("p (r x) -> p r x", x=STRIP)[:, quads[0] * QH:quads[1] * QH, :]
            if s == 0:
                return v.rearrange("p r (c s d) -> p r c s d", s=2, d=HD)[:, :, :, lo, :]
            return v.rearrange("p r (s c d) -> p r s c d", s=2, d=HD)[:, :, lo, :, :]

        def qkv_at(b, s):
            return (3, 2)[s] if b == 0 else 3 * b + (1, 3)[s]

        def flat(v):
            return v[:].rearrange("p a b -> p (a b)")

        W_OFF = [0, W1C, W1C + W2C]
        W_COLS = [W1C, W2C, W3C]
        W_STEPS = [c // SPLIT for c in W_COLS]

        def parts_read(m, e):
            return ((z_full, 16 * e + 12), (z_full, 16 * e + 16), (o_full, T * (e + 1)))[m]

        @block.sync
        def _(sp):
            sp.dma_start(x_sb[:, 0:TPB, :], x[0].rearrange("(j p) d -> p j d", p=P)).then_inc(x_in, 16)
            sp.dma_start(w_raw[:, 1], Wk.rearrange("(o p) d -> p o d", p=P)).then_inc(wk_in, 16)
            sp.dma_start(w_raw[:, 0], Wq.rearrange("(o p) d -> p o d", p=P)).then_inc(wq_in, 16)
            sp.wait_ge(rw_zeroed, 1)
            sp.dma_start(rw_sb[:, :, 0:E], rw.rearrange("(k p) e -> p k e", p=P)).then_inc(rw_in, 16)

            def load_expert(e):
                for m, (w, k, width) in enumerate(((w1, KD, I), (w2, KI, I), (w3, KI, D))):
                    if not (isinstance(e, int) and e == 0):
                        sp.wait_ge(w_hi_ready[m], e * W_STEPS[m])
                        sp.wait_ge(w_lo_ready[m], e * W_STEPS[m])
                    src = w[bass.ds(e, 1)].rearrange("a (k p) n -> p (a k) n", p=P)
                    dst = raw[:, W_OFF[m]:W_OFF[m] + W_COLS[m]].rearrange("p (k n) -> p k n", n=width)
                    sp.dma_start(dst, src).then_inc(w_in[m], 16)

            load_expert(0)
            for b in range(1, B):
                if b == 1:
                    sp.wait_ge(pro_full, 1)
                else:
                    sp.wait_ge(a_full, 5 * (b - 2) + 2)
                sp.dma_start(ctx_sb[:], ctx[b].rearrange("(j p) d -> p j d", p=P)).then_inc(ctx_in, 16)
            with sp.Fori(1, E) as e:
                load_expert(e)
            for t in range(T):
                sp.wait_ge(o_free, (E - 1) * T + t + 1)
                sp.dma_start(out[t // TPB, (t % TPB) * P:(t % TPB + 1) * P, :], acc[:, t, :]).then_inc(out_done, 16)
            sp.wait_ge(out_done, 16 * T)

        @block.gpsimd
        def _(pool):
            links = Links(pool, pool_step)
            pool.memset(rw_sb[:], 0.0).then_inc(rw_zeroed, 1)
            pool.memset(ident[:], 0.0).then_inc(pool_zeroed, 1)
            pool.wait_ge(pool_zeroed, 1)
            pool.affine_select(out=ident[:], in_=ident[:], compare_op=ALU.not_equal, fill=1.0, base=0,
                               pattern=[[-1, P]], channel_multiplier=1).then_inc(ident_ready, 1)
            links.after(pool.memset(v_ext[:], 0.0))
            pool.memset(v_ext[:, :, :, HD:HD + 1], 1.0).then_inc(v_const_ready, 1)
            links.after(pool.memset(before[:], 0.0))
            for i in range(1, E):
                pool.memset(before[:, i, 0:i], 1.0).then_inc(mask_ready, 1)

            def rsqrt(a, y, t, src, mul, eps, done):
                links.after(pool.tensor_scalar(a, src, mul, eps, ALU.mult, ALU.add))
                links.after(pool.tensor_scalar(y.bitcast(I32), a.bitcast(I32), -0.5, MAGIC, ALU.mult, ALU.add))
                for n in range(NEWTON):
                    links.after(pool.tensor_tensor(t, y, y, ALU.mult))
                    links.after(pool.tensor_tensor(t, t, a, ALU.mult))
                    links.after(pool.tensor_scalar(t, t, -0.5, 1.5, ALU.mult, ALU.add))
                    last = pool.tensor_tensor(y, y, t, ALU.mult)
                    if n < NEWTON - 1:
                        links.after(last)
                last.then_inc(done, 1)

            def norm1(t0, t1_, done):
                pool.wait_ge(mv1_ready, t1_)
                rsqrt(a1[:, t0:t1_], y1[:, t0:t1_], t1[:, t0:t1_], mv1[:, t0:t1_, 1], 1.0, LN_EPS, done)

            def round_qk(b):
                pool.wait_ge(b_full, Q * b)
                for s in (1, 0):
                    pool.wait_ge(normed, NORMS0 + 2 * (b - 1) + (2 - s))
                    pool.tensor_scalar(part(s, 0, ALL), twice(s, ALL), 1.0, 0.0, ALU.mult, ALU.add).then_inc(hi_ready, 1)

            def round_half(n, quads):
                pool.wait_ge(normed, 2 * n + 1)
                pool.tensor_scalar(part(1, 0, quads), twice(1, quads), 1.0, 0.0, ALU.mult, ALU.add).then_inc(k_hi_ready, 1)

            def values(b, half):
                pool.wait_ge(qkv_ready, qkv_at(b, 1))
                if b == 0:
                    pool.wait_ge(v_const_ready, 1)
                else:
                    pool.wait_ge(pv_done, Q * (b - 1) + Q // 2 * (half + 1))
                heads = slice(half * H // 2, (half + 1) * H // 2)
                for c in range(TPB):
                    v = kv_sb[:, c, :].rearrange("p (h d s) -> p h d s", d=HD, s=2)[:, heads, :, 1]
                    pool.tensor_scalar(v_ext[:, c, heads, 0:HD], v, 1.0, 0.0, ALU.mult, ALU.add).then_inc(v_ready, 1)

            def norm2(b):
                pool.wait_ge(mv2_ready, TPB * (b + 1))
                rsqrt(a2[:], y2[:], t2[:], mv2[:, :, 1], 1.0, LN_EPS, rstd2_ready)

            def split(m):
                pool.wait_ge(w_in[m], 16)
                for s in range(W_STEPS[m]):
                    cols = slice(W_OFF[m] + s * SPLIT, W_OFF[m] + (s + 1) * SPLIT)
                    pool.tensor_scalar(w_hi[:, cols], raw[:, cols], 1.0, 0.0, ALU.mult, ALU.add).then_inc(w_hi_ready[m], 1)

            norm1(0, TPB, rstd1_ready)
            norm1(TPB, T, rstd1_ready)
            round_half(0, FRONT)
            values(0, 0)
            round_half(1, BACK)
            values(0, 1)

            def step(b, first=False, last=False):
                if not first:
                    values(b, 1)
                    norm2(b - 1)
                if not last:
                    values(b + 1, 0)
                    round_qk(b + 1)

            step(0, first=True)
            for b in range(1, B):
                step(b, last=(b == B - 1))
            for m in range(3):
                split(m)
            norm2(B - 1)

        @block.scalar
        def _(act):
            act.dma_start(ctx_sb[:], ctx[0].rearrange("(j p) d -> p j d", p=P)).then_inc(ctx_in, 16)
            act.dma_start(w_raw[:, 2], Wv.rearrange("(o p) d -> p o d", p=P)).then_inc(wv_in, 16)
            act.dma_start(x_sb[:, TPB:, :].rearrange("p (b j) d -> p b j d", j=TPB),
                          x[1:].rearrange("b (j p) d -> p b j d", p=P)).then_inc(x_rest_in, 16)

            def hi_copy(dst, bank, sem, value):
                act.wait_ge(sem, value)
                act.activation(dst, bank[:], ACT.Copy).then_inc(hi_copied, 1)

            def copy_a(b, use, dst):
                if use == 2:
                    act.wait_ge(normed, NORMS0 + 2 * (b - 1))
                if use == 3:
                    act.wait_ge(v_ready, V_PARTS * b)
                act.wait_ge(a_full, 5 * (b - 1) + use + 1)
                act.activation(dst, bank_a[:], ACT.Copy).then_inc(qkv_ready, 1)

            def copy_pv(b, g):
                act.wait_ge(pv_done, Q * b + g + 1)
                if b > 0 and g in (0, 4):
                    act.wait_ge(c_full, C_USES * (b - 1) + (2 if g == 0 else 4))
                act.activation(oT[:, g, :], pv_bank[:, 0:N], ACT.Copy).then_inc(pv_free, 1)

            def step(b, last):
                for h in range(2 * Q):
                    g, pair = h // 2, h % 2
                    if pair == 0 and not (b == 0 and g < 2):
                        act.wait_ge(pv_done, Q * b + g - 1)
                    for r in (2 * pair, 2 * pair + 1):
                        act.wait_ge(s_full, HQ * (Q * b + g) + r + 1)
                        act.activation(probs[:, g % 2, r, :], s_bank[r][:], ACT.Exp, scale=SCALE).then_inc(exp_done, 1)
                    if pair == 1 and g > 0:
                        copy_pv(b, g - 1)
                    if pair == 1 and g == 0 and b > 0:
                        copy_pv(b - 1, Q - 1)
                    if b == 0 and h == 0:
                        round_q(BACK, 1)
                    if not last and h in PREP_AT:
                        use = PREP_AT.index(h)
                        if use < 2:
                            hi_copy(flat((xT_hi, cT_hi)[use]), bank_a, a_full, 5 * b + use + 1)
                        else:
                            copy_a(b + 1, use, flat(q_sb) if use == 2 else kv_sb[:, use - 3, :])
                if last:
                    copy_pv(b, Q - 1)

            def round_q(quads, n):
                act.wait_ge(normed, 2 * n + 2)
                act.activation(part(0, 0, quads), twice(0, quads), ACT.Copy).then_inc(q_hi_ready, 1)

            for n, (dst, bank) in enumerate(((cT_hi, bank_b), (wT_hi[:, 1], s_bank[0]), (wT_hi[:, 2], s_bank[1]), (wT_hi[:, 0], s_bank[2]))):
                hi_copy(dst[:].rearrange("p a b -> p (a b)"), bank, pro_full, n + 1)
            for n, (dst, bank) in enumerate(((kv_sb[:, 0, :], s_bank[3]), (None, None), (kv_sb[:, 1, :], pv_bank), (flat(q_sb), bank_c))):
                if dst is None:
                    hi_copy(flat(xT_hi), bank_a, pro_full, 6)
                    continue
                act.wait_ge(pro_full, 5 + n)
                act.activation(dst, bank[:], ACT.Copy).then_inc(qkv_ready, 1)
            round_q(FRONT, 0)
            for b in range(B):
                step(b, b == B - 1)

            def hidden(first, hi):
                for m in range(KI):
                    act.wait_ge(z_full, first + m + 1)
                    if not (isinstance(first, int) and first == 0):
                        act.wait_ge(h_ready, first + m - 3)
                    act.activation(silu[:, m, :], s_bank[m][:], ACT.Silu).then_inc(silu_ready, 1)
                    act.activation(hi[:, m, :], s_bank[m][:], ACT.Silu).then_inc(h_hi_ready, 1)

            def split(m, e):
                act.wait_ge(w_in[m], 16 * (e + 1))
                act.wait_ge(*parts_read(m, e - 1))
                for s in range(W_STEPS[m]):
                    cols = slice(W_OFF[m] + s * SPLIT, W_OFF[m] + (s + 1) * SPLIT)
                    act.activation(w_hi[:, cols], raw[:, cols], ACT.Copy).then_inc(w_hi_ready[m], 1)

            def expert(e, first=False, last=False):
                hidden(16 * e + 4, h2_hi)
                hidden(16 * e + 8, h1_hi)
                if first:
                    act.wait_ge(shifted, 1)
                    act.activation(pr[:], pr[:], ACT.Exp).then_inc(exped, 1)
                if not last:
                    split(0, e + 1)
                hidden(16 * e + 12, h2_hi)
                if not last:
                    hidden(16 * e + 16, h1_hi)
                    split(1, e + 1)
                    split(2, e + 1)

            hidden(0, h1_hi)
            expert(0, first=True)
            with act.Fori(1, E - 1) as e:
                expert(e)
            expert(E - 1, last=True)

        @block.vector
        def _(dve):
            links = Links(dve, dve_step)

            def lo_copy(dst, bank, hi, n):
                dve.wait_ge(hi_copied, n + 1)
                dve.tensor_tensor(dst, bank[:], hi.bitcast(F32), ALU.subtract).then_inc(xc_ready, 1)

            def x_norm(b):
                if b == 1:
                    dve.wait_ge(rstd1_ready, 2)
                for j in range(TPB):
                    t = TPB * b + j
                    dve.tensor_scalar(xn[:, j, :], x_sb[:, t, :],
                                      mv1[:, t, 0:1], y1[:, t:t + 1],
                                      ALU.subtract, ALU.mult).then_inc(xn_ready, 1)

            q_in = q_sb[:].rearrange("p j (g h d) -> p g j h d", h=HQ, d=HD)
            k_in = kv_sb[:].rearrange("p c (g h d s) -> p g c h d s", h=HQ, d=HD, s=2)[:, :, :, :, :, 0]

            def by_head(s, quads):
                return tmp[:, s, :].rearrange("p (g j h d) -> p g j h d", j=TPB, h=HQ, d=HD)[:, quads[0]:quads[1]]

            def heads(v, quads):
                return v[:, :, quads[0] * QH:quads[1] * QH]

            def squares(b, s, quads):
                dve.wait_ge(qkv_ready, qkv_at(b, s))
                if b > 0:
                    dve.wait_ge(parts_ready, NORMS0 + 2 * (b - 1))
                v = (q_in, k_in)[s][:, quads[0]:quads[1]]
                links.after(dve.tensor_tensor(by_head(s, quads), v, v, ALU.mult))
                return links.mark(dve.tensor_reduce(ssq[:, s, quads[0] * QH:quads[1] * QH], rows_of(tmp[:, s, :], quads), AX, ALU.add))

            def rms_start(quads):
                a, y = heads(a3, quads), heads(y3, quads)
                links.after(dve.tensor_scalar(a, heads(ssq, quads), 1.0 / HD, RMS_EPS, ALU.mult, ALU.add))
                links.after(dve.tensor_scalar(y.bitcast(I32), a.bitcast(I32), -0.5, MAGIC, ALU.mult, ALU.add))

            def rms_newton(quads):
                a, y, t = heads(a3, quads), heads(y3, quads), heads(t3, quads)
                links.after(dve.tensor_tensor(t, y, y, ALU.mult))
                links.after(dve.scalar_tensor_tensor(t, t, -0.5, a, ALU.mult, ALU.mult))
                links.after(dve.scalar_tensor_tensor(y, t, 1.5, y, ALU.add, ALU.mult))

            def normalize(s, quads):
                n = quads[1] - quads[0]
                r = y3[:, s, :].rearrange("p (g j h) -> p g j h", j=TPB, h=HQ)[:, quads[0]:quads[1]]
                dve.tensor_tensor(by_head(s, quads), (q_in, k_in)[s][:, quads[0]:quads[1]],
                                  r.unsqueeze(4).to_broadcast([P, n, TPB, HQ, HD]), ALU.mult).then_inc(normed, 1)

            def part_lo(s, quads, sem, value):
                dve.wait_ge(sem, value)
                dve.tensor_tensor(part(s, 1, quads), twice(s, quads), part(s, 0, quads).bitcast(F32),
                                  ALU.subtract).then_inc(parts_ready, 1)

            def evac_b(b, g):
                dve.wait_ge(b_full, Q * b + g + 1)
                if b > 0:
                    dve.wait_ge(s_full, HQ * (Q * (b - 1) + g + 1))
                dve.tensor_copy(qkT[g // 4][:, g % 4, :], bank_b[:]).then_inc(b_free, 1)

            def divide(b, half, j):
                use = 2 * half + j
                dve.wait_ge(c_full, C_USES * b + use + 1)
                o = bank_c[:].rearrange("p (h s) -> p h s", s=STRIP)
                links.after(dve.reciprocal(r_den[:, use, :], o[:, :, HD]))
                dst = att[:, j, half * P:(half + 1) * P].rearrange("p (h d) -> p h d", d=HD)
                den = r_den[:, use, :].unsqueeze(2).to_broadcast([P, H // 2, HD])
                dve.tensor_tensor(dst, o[:, :, 0:HD], den, ALU.mult).then_inc(c_free, 1)

            def residual(b):
                dve.wait_ge(c_free, C_USES * b + 4)
                tiles = slice(TPB * b, TPB * (b + 1))
                done = links.mark(dve.tensor_tensor(acc[:, tiles, :], att[:], x_sb[:, tiles, :], ALU.add))
                links.wait(done)
                for j in range(TPB):
                    done = links.mark(dve.bn_stats(stats2[:, j, :], acc[:, TPB * b + j, :]))
                links.wait(done)
                for j in range(TPB):
                    dve.bn_aggr(mv2[:, j, :], stats2[:, j, :]).then_inc(mv2_ready, 1)

            def x2_norm(b):
                dve.wait_ge(rstd2_ready, b + 1)
                for j in range(TPB):
                    dve.tensor_scalar(x2n[:, j, :], acc[:, TPB * b + j, :],
                                      mv2[:, j, 0:1], y2[:, j:j + 1], ALU.subtract, ALU.mult).then_inc(x2n_ready, 1)

            def x2_parts(b):
                dve.wait_ge(c_full, C_USES * b + 5)
                cols = slice(N * b, N * (b + 1))
                full = bank_c[:].rearrange("p (k n) -> p k n", k=KD)
                links.after(dve.tensor_copy(x2T_hi[:, :, cols], full))
                dve.tensor_tensor(x2T_lo[:, :, cols], full, x2T_hi[:, :, cols].bitcast(F32), ALU.subtract).then_inc(c_free, 1)

            def split(m, e):
                dve.wait_ge(w_in[m], 16 * (e + 1))
                if not (isinstance(e, int) and e == 0):
                    dve.wait_ge(*parts_read(m, e - 1))
                for s in range(W_STEPS[m]):
                    cols = slice(W_OFF[m] + s * SPLIT, W_OFF[m] + (s + 1) * SPLIT)
                    dve.wait_ge(w_hi_ready[m], W_STEPS[m] * e + s + 1)
                    dve.tensor_tensor(w_lo[:, cols], raw[:, cols], w_hi[:, cols].bitcast(F32),
                                      ALU.subtract).then_inc(w_lo_ready[m], 1)

            def step(b, first=False, last=False):
                for h in range(2 * Q):
                    if h in QK_AT:
                        evac_b(b, QK_AT.index(h) + 1)
                    if first and h == 0:
                        normalize(1, BACK)
                        normalize(0, BACK)
                    if first and h == 2:
                        part_lo(1, BACK, k_hi_ready, 2)
                        part_lo(0, BACK, q_hi_ready, 2)
                    if not first:
                        if h in O_AT:
                            use = O_AT.index(h)
                            divide(b - 1, use // 2, use % 2)
                        if h == 4:
                            residual(b - 1)
                    if last:
                        if h == 9:
                            x2_norm(b - 1)
                        if h == 11:
                            x2_parts(b - 1)
                        if h in (8, 9, 10):
                            split(h - 8, 0)
                        if h in (13, 14):
                            divide(b, 0, h - 13)
                        continue
                    if h == 0:
                        lo_copy(flat(xT_lo), bank_a, flat(xT_hi), XC0 + 2 * b)
                    if h == 1:
                        lo_copy(flat(cT_lo), bank_a, flat(cT_hi), XC0 + 2 * b + 1)
                    if h == 3:
                        q_done = squares(b + 1, 0, ALL)
                    if h == 6:
                        k_done = squares(b + 1, 1, ALL)
                        links.wait(max(k_done, q_done))
                        rms_start(ALL)
                    if h in (7, 8, 9):
                        rms_newton(ALL)
                    if h == 10:
                        normalize(1, ALL)
                        normalize(0, ALL)
                    if h == 11 and not first:
                        x2_norm(b - 1)
                    if h == 12:
                        part_lo(1, ALL, hi_ready, 2 * b + 1)
                    if h == 13:
                        part_lo(0, ALL, hi_ready, 2 * b + 2)
                    if h == 14:
                        evac_b(b + 1, 0)
                        if not first:
                            x2_parts(b - 1)
                        if b + 2 < B:
                            x_norm(b + 2)

            def stats(t0, t1_):
                dve.wait_ge(x_in if t0 == 0 else x_rest_in, 16)
                for t in range(t0, t1_):
                    done = links.mark(dve.bn_stats(stats1[:, t, :], x_sb[:, t, :]))
                links.wait(done)
                for t in range(t0, t1_):
                    dve.bn_aggr(mv1[:, t, :], stats1[:, t, :]).then_inc(mv1_ready, 1)

            stats(0, TPB)
            for n, (lo, bank, hi) in enumerate(((cT_lo, bank_b, cT_hi), (wT_lo[:, 1], s_bank[0], wT_hi[:, 1]), (wT_lo[:, 2], s_bank[1], wT_hi[:, 2]))):
                lo_copy(flat(lo), bank, flat(hi), n)
            dve.wait_ge(rstd1_ready, 1)
            x_norm(0)
            lo_copy(flat(wT_lo[:, 0]), s_bank[2], flat(wT_hi[:, 0]), 3)
            lo_copy(flat(xT_lo), bank_a, flat(xT_hi), 4)
            stats(TPB, T)
            dve.wait_ge(rw_in, 16)
            links.after(dve.tensor_copy(rw_hi[:], rw_sb[:]))
            dve.tensor_tensor(rw_lo[:], rw_sb[:], rw_hi[:].bitcast(F32), ALU.subtract).then_inc(rw_split, 1)
            squares(0, 1, ALL)
            links.wait(squares(0, 0, ALL))
            rms_start(ALL)
            for _ in range(NEWTON):
                rms_newton(ALL)
            normalize(1, FRONT)
            normalize(0, FRONT)
            part_lo(1, FRONT, k_hi_ready, 1)
            part_lo(0, FRONT, q_hi_ready, 1)
            evac_b(0, 0)
            x_norm(1)

            step(0, first=True)
            for b in range(1, B):
                step(b, last=(b == B - 1))

            def hidden(first, hi, lo, chunks=range(KI)):
                for m in chunks:
                    dve.wait_ge(silu_ready, first + m + 1)
                    dve.wait_ge(h_hi_ready, first + m + 1)
                    dve.tensor_tensor(lo[:, m, :], silu[:, m, :], hi[:, m, :].bitcast(F32), ALU.subtract).then_inc(h_ready, 1)

            def combine(e, t):
                for j in range(HT):
                    tile = HT * t + j
                    dve.wait_ge(o_full, T * e + tile + 1)
                    dve.scalar_tensor_tensor(acc[:, tile, :], out_bank[j][:, 0:D], gates[:, tile, bass.ds(e, 1)],
                                             acc[:, tile, :], ALU.mult, ALU.add).then_inc(o_free, 1)

            def expert(e, first=False, last=False):
                if first:
                    hidden(4, h2_hi, h2_lo, range(1))
                    x2_parts(B - 1)
                    hidden(4, h2_hi, h2_lo, range(1, KI))
                else:
                    hidden(16 * e + 4, h2_hi, h2_lo)
                hidden(16 * e + 8, h1_hi, h1_lo)
                if first:
                    router()
                if not last:
                    split(0, e + 1)
                combine(e, 0)
                hidden(16 * e + 12, h2_hi, h2_lo)
                if not last:
                    hidden(16 * e + 16, h1_hi, h1_lo)
                    split(1, e + 1)
                combine(e, 1)
                if not last:
                    split(2, e + 1)

            def router():
                le = [P, T, E]
                for half in range(2):
                    dve.wait_ge(c_full, C_USES * B + half + 1)
                    dve.tensor_copy(logT[0:E, half * HALF:(half + 1) * HALF], (bank_b, bank_c)[half][0:E, :]).then_inc(c_free, 1)
                dve.wait_ge(c_full, C_USES * B + 3)
                dve.tensor_copy(flat(logits), bank_c[:, 0:T * E]).then_inc(c_free, 1)
                dve.wait_ge(c_free, C_USES * B + 3)
                links.after(dve.tensor_reduce(row[:, 0, :], logits[:], AX, ALU.max))
                dve.tensor_tensor(pr[:], logits[:], row[:, 0, :].unsqueeze(2).to_broadcast(le), ALU.subtract).then_inc(shifted, 1)
                dve.wait_ge(exped, 1)
                links.after(dve.tensor_reduce(row[:, 1, :], pr[:], AX, ALU.add))
                links.after(dve.reciprocal(row[:, 2, :], row[:, 1, :]))
                links.after(dve.tensor_tensor(pr[:], pr[:], row[:, 2, :].unsqueeze(2).to_broadcast(le), ALU.mult))
                other = pr[:].unsqueeze(2).to_broadcast([P, T, E, E])
                own = pr[:].unsqueeze(3).to_broadcast([P, T, E, E])
                v4 = lambda m: m[:].rearrange("p (t i) j -> p t i j", i=E)
                links.mark(dve.tensor_tensor(v4(gt), other, own, ALU.is_gt))
                links.after(dve.tensor_tensor(v4(eq), other, own, ALU.is_equal))
                dve.wait_ge(mask_ready, E - 1)
                links.after(dve.tensor_tensor(v4(eq), v4(eq), before[:].unsqueeze(1).to_broadcast([P, T, E, E]), ALU.mult))
                links.after(dve.tensor_tensor(gt[:], gt[:], eq[:], ALU.add))
                g = flat(gates)
                links.after(dve.tensor_reduce(g, gt[:], AX, ALU.add))
                links.after(dve.tensor_scalar(g, g, float(TOP), None, ALU.is_lt))
                links.after(dve.tensor_tensor(pr[:], pr[:], gates[:], ALU.mult))
                links.after(dve.tensor_reduce(row[:, 3, :], pr[:], AX, ALU.add))
                links.after(dve.reciprocal(row[:, 1, :], row[:, 3, :]))
                links.after(dve.tensor_tensor(gates[:], pr[:], row[:, 1, :].unsqueeze(2).to_broadcast(le), ALU.mult))

            hidden(0, h1_hi, h1_lo, (0,))
            divide(B - 1, 1, 0)
            hidden(0, h1_hi, h1_lo, (1,))
            divide(B - 1, 1, 1)
            residual(B - 1)
            hidden(0, h1_hi, h1_lo, (2, 3))
            x2_norm(B - 1)
            expert(0, first=True)
            with dve.Fori(1, E - 1) as e:
                expert(e)
            expert(E - 1, last=True)

        @block.tensor
        def _(pe):
            def transpose(bank, src):
                for j in range(TPB):
                    for c in range(KD):
                        last = pe.transpose(bank[:, c * N + j * P:c * N + (j + 1) * P], src[:, j, c * P:(c + 1) * P], ident[:])
                return last

            def project(bank_cols, hi, lo, tok, w0, w1_):
                for k in range(KD):
                    for i, (v, w) in enumerate(((hi, wT_hi), (hi, wT_lo), (lo, wT_hi))):
                        last = pe.matmul(bank_cols, v[:, k, tok], w[:, w0:w1_, k, :], start=(k == 0 and i == 0),
                                         stop=(k == KD - 1 and i == 2))
                return last

            def project_kv(bank, c):
                return project(bank[:], cT_hi, cT_lo, slice(c * P, (c + 1) * P), 1, 3)

            def project_q(bank):
                for j in range(TPB):
                    last = project(bank[:, j * D:(j + 1) * D], xT_hi, xT_lo, slice(j * P, (j + 1) * P), 0, 1)
                return last

            def prep(b, use):
                if use == 0:
                    pe.wait_ge(qkv_ready, 3 * b)
                    pe.wait_ge(xn_ready, TPB * (b + 1))
                    last = transpose(bank_a, xn)
                elif use == 1:
                    pe.wait_ge(xc_ready, XC0 + 2 * b - 1)
                    pe.wait_ge(ctx_in, 16 * (b + 1))
                    last = transpose(bank_a, ctx_sb)
                elif use == 2:
                    pe.wait_ge(xc_ready, XC0 + 2 * b)
                    last = project_q(bank_a)
                else:
                    pe.wait_ge(qkv_ready, 3 * b + use - 2)
                    last = project_kv(bank_a, use - 3)
                last.then_inc(a_full, 1)

            def qk_transpose(b, g):
                if g == 0:
                    pe.wait_ge(parts_ready, 2 if b == 0 else NORMS0 + 2 * b)
                if b == 0 and g == Q // 2:
                    pe.wait_ge(parts_ready, NORMS0)
                if not (b == 0 and g == 0):
                    pe.wait_ge(b_free, Q * b + g)
                for s in range(2):
                    for j in range(TPB):
                        v = qk_part[s][:, (TPB * g + j) * P:(TPB * g + j + 1) * P].bitcast(F32)
                        last = pe.transpose(bank_b[:, s * N + j * P:s * N + (j + 1) * P], v, ident[:])
                last.then_inc(b_full, 1)

            def scores(b, g, pair):
                if pair == 0:
                    pe.wait_ge(b_free, Q * b + g + 1)
                for c in range(TPB):
                    for r in (2 * pair, 2 * pair + 1):
                        if c == 0 and not (b == 0 and g == 0):
                            pe.wait_ge(exp_done, HQ * (Q * b + g - 1) + r + 1)
                        rows = slice(STRIP * r, STRIP * (r + 1))
                        qk = qkT[g // 4][rows, g % 4, :]
                        last = pe.matmul(s_bank[r][:, c * N:(c + 1) * N], qk[:, N + c * P:N + (c + 1) * P], qk[:, 0:N],
                                         start=True, stop=True)
                        if c == TPB - 1:
                            last.then_inc(s_full, 1)

            def values(b, g, c):
                if c == 0:
                    if g % (Q // 2) == 0:
                        pe.wait_ge(v_ready, V_PARTS * b + TPB * (1 + g // (Q // 2)))
                    if not (b == 0 and g == 0):
                        pe.wait_ge(pv_free, Q * b + g)
                    pe.wait_ge(exp_done, HQ * (Q * b + g + 1))
                for r in range(HQ):
                    rows = slice(STRIP * r, STRIP * (r + 1))
                    last = pe.matmul(pv_bank[rows, 0:N], v_ext[:, c, HQ * g + r, :], probs[:, g % 2, r, c * N:(c + 1) * N],
                                     start=(c == 0), stop=(c == TPB - 1), tile_position=(0, STRIP * r))
                if c == TPB - 1:
                    last.then_inc(pv_done, 1)

            def before_c(u):
                if u > 0:
                    pe.wait_ge(c_free, u)

            def o_transpose(b, half, j):
                before_c(C_USES * b + 2 * half + j)
                pe.wait_ge(pv_free, Q * b + 4 * (half + 1))
                for g in range(4):
                    last = pe.transpose(bank_c[:, g * P:(g + 1) * P], oT[:, 4 * half + g, j * P:(j + 1) * P], ident[:])
                last.then_inc(c_full, 1)

            def x2_transpose(b):
                pe.wait_ge(x2n_ready, TPB * (b + 1))
                before_c(C_USES * b + 4)
                for j in range(TPB):
                    for k in range(KD):
                        last = pe.transpose(bank_c[:, k * N + j * P:k * N + (j + 1) * P], x2n[:, j, k * P:(k + 1) * P], ident[:])
                last.then_inc(c_full, 1)

            def weights(m, k, width, first, cols):
                at = slice(W_OFF[m] + k * width + first, W_OFF[m] + k * width + first + cols)
                return w_hi[:, at], w_lo[:, at]

            def layer(m, e, t, chunk, rhs_hi, rhs_lo, ks, cols, chunks=range(KI)):
                for n in chunks:
                    if isinstance(chunk, int) and chunk == 0:
                        pe.wait_ge(exp_done, HQ * (Q * B - 1) + n + 1)
                    else:
                        pe.wait_ge(h_hi_ready, chunk + n - 3)
                    for k in range(ks):
                        if m == 1 and n == 0:
                            pe.wait_ge(h_ready, chunk + k - 3)
                        hi, lo = weights(m, k, I, n * P, P)
                        for i, (w, r) in enumerate(((hi, rhs_hi), (hi, rhs_lo), (lo, rhs_hi))):
                            last = pe.matmul(s_bank[n][:], w, r[:, k, cols], start=(k == 0 and i == 0),
                                             stop=(k == ks - 1 and i == 2))
                    last.then_inc(z_full, 1)

            def layer1(e, t, chunks=range(KI)):
                if t == 0 and 0 in chunks:
                    pe.wait_ge(w_lo_ready[0], W_STEPS[0] * (e + 1))
                layer(0, e, t, 16 * e + 8 * t, x2T_hi, x2T_lo, KD, slice(t * HALF, (t + 1) * HALF), chunks)

            def step(b, first=False, last=False):
                for h in range(2 * Q):
                    g, pair = h // 2, h % 2
                    scores(b, g, pair)
                    if h in QK_AT:
                        qk_transpose(b, QK_AT.index(h) + 1)
                    if not last and h == 14:
                        qk_transpose(b + 1, 0)
                    if g > 0:
                        values(b, g - 1, pair)
                    elif not first:
                        values(b - 1, Q - 1, pair)
                    if not first and h in O_AT:
                        use = O_AT.index(h)
                        o_transpose(b - 1, use // 2, use % 2)
                    if not first and h == (11 if last else 13):
                        x2_transpose(b - 1)
                    if last and h in (13, 14):
                        o_transpose(b, 0, h - 13)
                    if not last and h in PREP_AT:
                        prep(b + 1, PREP_AT.index(h))
                if last:
                    layer1(0, 0, (0,))
                    values(b, Q - 1, 0)
                    values(b, Q - 1, 1)

            def keep_warm(n):
                for _ in range(n):
                    pe.transpose(s_bank[0][:, 0:P], ident[:], ident[:])

            pe.wait_ge(ident_ready, 1)
            keep_warm(WARM)
            for bank, src, arrived, value in ((bank_b, ctx_sb, ctx_in, 16), (s_bank[0], w_raw[:, 1], wk_in, 16),
                                              (s_bank[1], w_raw[:, 2], wv_in, 16), (s_bank[2], w_raw[:, 0], wq_in, 16)):
                pe.wait_ge(arrived, value)
                transpose(bank, src).then_inc(pro_full, 1)
            pe.wait_ge(xc_ready, 3)
            project_kv(s_bank[3], 0).then_inc(pro_full, 1)
            pe.wait_ge(xn_ready, TPB)
            transpose(bank_a, xn).then_inc(pro_full, 1)
            project_kv(pv_bank, 1).then_inc(pro_full, 1)
            pe.wait_ge(xc_ready, XC0)
            project_q(bank_c).then_inc(pro_full, 1)
            keep_warm(WARM)
            pe.wait_ge(normed, 1)
            keep_warm(WARM)
            qk_transpose(0, 0)
            step(0, first=True)
            for b in range(1, B):
                step(b, last=(b == B - 1))

            def layer2(e, t, chunks=range(KI)):
                if t == 0 and 0 in chunks:
                    pe.wait_ge(w_lo_ready[1], W_STEPS[1] * (e + 1))
                layer(1, e, t, 16 * e + 8 * t + 4, h1_hi, h1_lo, KI, slice(0, HALF), chunks)

            def layer3(e, t, tiles=range(HT), ks=range(KI)):
                if t == 0 and 0 in tiles:
                    pe.wait_ge(w_lo_ready[2], W_STEPS[2] * (e + 1))
                for j in tiles:
                    n = T * e + HT * t + j
                    if not (isinstance(n, int) and n < HT) and ks[0] == 0:
                        pe.wait_ge(o_free, n - HT + 1)
                    for k in ks:
                        if j == 0:
                            pe.wait_ge(h_ready, 16 * e + 8 * t + 4 + k + 1)
                        whi, wlo = weights(2, k, D, 0, D)
                        tok = slice(j * P, (j + 1) * P)
                        for i, (h, w) in enumerate(((h2_hi, whi), (h2_hi, wlo), (h2_lo, whi))):
                            last = pe.matmul(out_bank[j][:, 0:D], h[:, k, tok], w, start=(k == 0 and i == 0),
                                             stop=(k == KI - 1 and i == 2))
                    if ks[-1] == KI - 1:
                        last.then_inc(o_full, 1)

            def router():
                pe.wait_ge(rw_split, 1)
                for half in range(2):
                    for k in range(KD):
                        for i, (w, r) in enumerate(((rw_hi, x2T_hi), (rw_hi, x2T_lo), (rw_lo, x2T_hi))):
                            last = pe.matmul((bank_b, bank_c)[half][:], w[:, k, :], r[:, k, half * HALF:(half + 1) * HALF],
                                             start=(k == 0 and i == 0), stop=(k == KD - 1 and i == 2))
                    last.then_inc(c_full, 1)

            def router_transpose():
                before_c(C_USES * B + 2)
                for t in range(T):
                    last = pe.transpose(bank_c[:, t * E:(t + 1) * E], logT[0:E, t * P:(t + 1) * P], ident[0:E, 0:E])
                last.then_inc(c_full, 1)

            def expert(e, first=False, last=False):
                if first:
                    layer2(e, 0, range(2))
                    x2_transpose(B - 1)
                    layer2(e, 0, range(2, KI))
                    before_c(C_USES * B)
                else:
                    layer2(e, 0)
                layer1(e, 1)
                if first:
                    router()
                    layer3(e, 0, (0, 1))
                    router_transpose()
                    layer3(e, 0, (2,))
                    before_c(C_USES * B + 3)
                    layer3(e, 0, (3,))
                else:
                    layer3(e, 0)
                layer2(e, 1)
                if last:
                    layer3(e, 1, ks=range(KI - 1))
                    layer3(e, 1, ks=(KI - 1,))
                else:
                    layer1(e + 1, 0)
                    layer3(e, 1)

            layer1(0, 0, (1,))
            o_transpose(B - 1, 1, 0)
            layer1(0, 0, (2,))
            o_transpose(B - 1, 1, 1)
            layer1(0, 0, (3,))
            expert(0, first=True)
            with pe.Fori(1, E - 1) as e:
                expert(e)
            expert(E - 1, last=True)


_INS = ['x', 'ctx_2048', 'L0_xattn_Wq', 'L0_xattn_Wk', 'L0_xattn_Wv', 'L0_ffn_router_w', 'L0_ffn_w1', 'L0_ffn_w2', 'L0_ffn_w3']


def kernel(**inputs):
    import numpy as np
    import concourse.bacc as bacc
    from concourse.bass_utils import run_bass_kernel_spmd

    nc = bacc.Bacc("TRN2", target_bir_lowering=False, num_devices=1)
    arrays, args = {}, []
    for name in _INS:
        a = np.ascontiguousarray(inputs[name])
        arrays[f"in_{name}"] = a
        args.append(nc.dram_tensor(f"in_{name}", a.shape, mybir.dt.from_np(a.dtype), kind="ExternalInput").ap())
    out = nc.dram_tensor("out", (B, N, D), F32, kind="ExternalOutput").ap()
    build(nc, *args, out)
    result = run_bass_kernel_spmd(nc, [arrays], core_ids=[0])
    return result.results[0]["out"]
```
